# Optimizing a Trainium2 kernel written in Bass

```python
import numpy as np
import jax
import jax.numpy as jnp

def _softmax(x, axis=-1):
    return jax.nn.softmax(x, axis=axis)

def _gelu(x):
    return jax.nn.gelu(x, approximate=True)

def _silu(x):
    return jax.nn.silu(x)

def _sigmoid(x):
    return jax.nn.sigmoid(x)

def _layernorm(x, axis=-1, eps=1e-05):
    m = jnp.mean(x, axis=axis, keepdims=True)
    v = jnp.var(x, axis=axis, keepdims=True)
    return (x - m) / jnp.sqrt(v + eps)

def _scatter_add(tgt, idx, src, axis=0):
    return tgt.at[idx].add(src)

def _segment_sum(src, seg, n):
    return jax.ops.segment_sum(src, seg, n)
kernel_name = 'mk_macaron_d1_jaxref_r4_6fc6ba'

def setup_inputs(seed: int=0):
    np.random.seed(seed)
    _w = jnp.asarray

    def _L0_attn_setup():
        import jax, jax.numpy as jnp
        import numpy as np
        B, N, DIM, H = (4, 1024, 256, 16)
        HD = DIM // H
        SCALE = HD ** (-0.5)

        def _heads(t, bsz, ntok):
            return t.reshape(bsz, ntok, H, HD).transpose(0, 2, 1, 3)

        def _fwd(x, q_w1, q_b1, q_w2, q_b2, k_w1, k_b1, k_w2, k_b2, v_w, v_b, g_w, g_b, p_w, p_b):
            bsz, ntok, dim = x.shape
            gelu = lambda t: jax.nn.gelu(t, approximate=False)
            q = _heads(jax.nn.softplus(gelu(x @ q_w1.T + q_b1) @ q_w2.T + q_b2), bsz, ntok)
            k = _heads(jax.nn.softplus(gelu(x @ k_w1.T + k_b1) @ k_w2.T + k_b2), bsz, ntok)
            v = _heads(gelu(x @ v_w.T + v_b), bsz, ntok)
            g = _heads(gelu(x @ g_w.T + g_b), bsz, ntok)
            z = jnp.einsum('bhcn,bhc->bhn', q, k.sum(axis=-1)) * SCALE
            z = 1.0 / (z + dim)
            A = jnp.einsum('bhcn,bhcm->bhnm', q, k)
            out = jnp.einsum('bhnm,bhdm->bhdn', A, v) * SCALE
            out = (out + v) * z[:, :, None, :]
            out = out.reshape(bsz, ntok, dim)
            out = out * g.reshape(bsz, ntok, dim)
            return out @ p_w.T + p_b
        key = jax.random.key(seed)
        ks = jax.random.split(key, 16)
        w = lambda k: jax.random.normal(k, (DIM, DIM), jnp.float32) * 0.02
        b = lambda k: jax.random.normal(k, (DIM,), jnp.float32) * 0.02
        return {'x': jax.random.normal(ks[0], (B, N, DIM), jnp.float32), 'q_w1': w(ks[1]), 'q_b1': b(ks[2]), 'q_w2': w(ks[3]), 'q_b2': b(ks[4]), 'k_w1': w(ks[5]), 'k_b1': b(ks[6]), 'k_w2': w(ks[7]), 'k_b2': b(ks[8]), 'v_w': w(ks[9]), 'v_b': b(ks[10]), 'g_w': w(ks[11]), 'g_b': b(ks[12]), 'p_w': w(ks[13]), 'p_b': b(ks[14])}
    _L0_attn_in = _L0_attn_setup()

    def _L0_ffn_setup():
        import jax, jax.numpy as jnp
        import numpy as np
        B, S, H = (1, 512, 256)
        E, K = (16, 4)
        G, TG = (4, 2)
        I_MOE = 128
        N_SH = 2
        SCALE = 2.5

        def _mlp(x, gw, uw, dw):
            return jax.nn.silu(x @ gw.T) * (x @ uw.T) @ dw.T

        def _route(x2d, router_weight, e_bias):
            T = x2d.shape[0]
            scores = jax.nn.sigmoid(x2d @ router_weight.T)
            sc = scores + e_bias[None, :]
            group_scores = jnp.sum(jax.lax.top_k(sc.reshape(T, G, E // G), 2)[0], axis=-1)
            _, gidx = jax.lax.top_k(group_scores, TG)
            gmask = jnp.zeros((T, G), sc.dtype).at[jnp.arange(T)[:, None], gidx].set(1.0)
            smask = jnp.repeat(gmask, E // G, axis=1)
            masked = jnp.where(smask > 0, sc, 0.0)
            _, tidx = jax.lax.top_k(masked, K)
            tw = jnp.take_along_axis(scores, tidx, axis=1)
            tw = tw / (jnp.sum(tw, axis=-1, keepdims=True) + 1e-20)
            tw = tw * SCALE
            return (tidx, tw)

        def _moe_forward(hidden_states, router_weight, e_bias, gate_w, up_w, down_w, sh_gate_w, sh_up_w, sh_down_w):
            orig_shape = hidden_states.shape
            x = hidden_states.reshape(-1, H)
            T = x.shape[0]
            tidx, tw = _route(x, router_weight, e_bias)
            g = jnp.einsum('th,eih->tei', x, gate_w)
            u = jnp.einsum('th,eih->tei', x, up_w)
            h = jax.nn.silu(g) * u
            yo = jnp.einsum('tei,ehi->teh', h, down_w)
            combine = jnp.zeros((T, E), tw.dtype).at[jnp.arange(T)[:, None], tidx].add(tw)
            routed = jnp.einsum('te,teh->th', combine, yo)
            shared = _mlp(hidden_states.reshape(-1, H), sh_gate_w, sh_up_w, sh_down_w)
            return (routed + shared).reshape(orig_shape)
        key = jax.random.key(seed)
        ks = jax.random.split(key, 9)
        s = 0.02
        return {'hidden_states': jax.random.normal(ks[0], (B, S, H), jnp.float32), 'router_weight': jax.random.normal(ks[1], (E, H), jnp.float32) * s, 'e_bias': jnp.zeros((E,), jnp.float32), 'gate_w': jax.random.normal(ks[2], (E, I_MOE, H), jnp.float32) * s, 'up_w': jax.random.normal(ks[3], (E, I_MOE, H), jnp.float32) * s, 'down_w': jax.random.normal(ks[4], (E, H, I_MOE), jnp.float32) * s, 'sh_gate_w': jax.random.normal(ks[5], (N_SH * I_MOE, H), jnp.float32) * s, 'sh_up_w': jax.random.normal(ks[6], (N_SH * I_MOE, H), jnp.float32) * s, 'sh_down_w': jax.random.normal(ks[7], (H, N_SH * I_MOE), jnp.float32) * s}
    _L0_ffn_in = _L0_ffn_setup()
    _d = {'L0_attn_x': _L0_attn_in['x'], 'L0_attn_q_w1': _L0_attn_in['q_w1'], 'L0_attn_q_b1': _L0_attn_in['q_b1'], 'L0_attn_q_w2': _L0_attn_in['q_w2'], 'L0_attn_q_b2': _L0_attn_in['q_b2'], 'L0_attn_k_w1': _L0_attn_in['k_w1'], 'L0_attn_k_b1': _L0_attn_in['k_b1'], 'L0_attn_k_w2': _L0_attn_in['k_w2'], 'L0_attn_k_b2': _L0_attn_in['k_b2'], 'L0_attn_v_w': _L0_attn_in['v_w'], 'L0_attn_v_b': _L0_attn_in['v_b'], 'L0_attn_g_w': _L0_attn_in['g_w'], 'L0_attn_g_b': _L0_attn_in['g_b'], 'L0_attn_p_w': _L0_attn_in['p_w'], 'L0_attn_p_b': _L0_attn_in['p_b'], 'L0_ffn_router_weight': _L0_ffn_in['router_weight'], 'L0_ffn_e_bias': _L0_ffn_in['e_bias'], 'L0_ffn_gate_w': _L0_ffn_in['gate_w'], 'L0_ffn_up_w': _L0_ffn_in['up_w'], 'L0_ffn_down_w': _L0_ffn_in['down_w'], 'L0_ffn_sh_gate_w': _L0_ffn_in['sh_gate_w'], 'L0_ffn_sh_up_w': _L0_ffn_in['sh_up_w'], 'L0_ffn_sh_down_w': _L0_ffn_in['sh_down_w']}
    _x0 = _d['L0_attn_x']
    _d['L0_attn_x'] = jax.random.normal(jax.random.fold_in(jax.random.key(seed), 1), (16, 512, 256), dtype=_x0.dtype)
    del _x0
    return _d

def reference(L0_attn_x, L0_attn_q_w1, L0_attn_q_b1, L0_attn_q_w2, L0_attn_q_b2, L0_attn_k_w1, L0_attn_k_b1, L0_attn_k_w2, L0_attn_k_b2, L0_attn_v_w, L0_attn_v_b, L0_attn_g_w, L0_attn_g_b, L0_attn_p_w, L0_attn_p_b, L0_ffn_router_weight, L0_ffn_e_bias, L0_ffn_gate_w, L0_ffn_up_w, L0_ffn_down_w, L0_ffn_sh_gate_w, L0_ffn_sh_up_w, L0_ffn_sh_down_w):

    def _L0_attn_ref(x, q_w1, q_b1, q_w2, q_b2, k_w1, k_b1, k_w2, k_b2, v_w, v_b, g_w, g_b, p_w, p_b):
        import jax, jax.numpy as jnp
        import numpy as np
        B, N, DIM, H = (4, 1024, 256, 16)
        HD = DIM // H
        SCALE = HD ** (-0.5)

        def _heads(t, bsz, ntok):
            return t.reshape(bsz, ntok, H, HD).transpose(0, 2, 1, 3)

        def _fwd(x, q_w1, q_b1, q_w2, q_b2, k_w1, k_b1, k_w2, k_b2, v_w, v_b, g_w, g_b, p_w, p_b):
            bsz, ntok, dim = x.shape
            gelu = lambda t: jax.nn.gelu(t, approximate=False)
            q = _heads(jax.nn.softplus(gelu(x @ q_w1.T + q_b1) @ q_w2.T + q_b2), bsz, ntok)
            k = _heads(jax.nn.softplus(gelu(x @ k_w1.T + k_b1) @ k_w2.T + k_b2), bsz, ntok)
            v = _heads(gelu(x @ v_w.T + v_b), bsz, ntok)
            g = _heads(gelu(x @ g_w.T + g_b), bsz, ntok)
            z = jnp.einsum('bhcn,bhc->bhn', q, k.sum(axis=-1)) * SCALE
            z = 1.0 / (z + dim)
            A = jnp.einsum('bhcn,bhcm->bhnm', q, k)
            out = jnp.einsum('bhnm,bhdm->bhdn', A, v) * SCALE
            out = (out + v) * z[:, :, None, :]
            out = out.reshape(bsz, ntok, dim)
            out = out * g.reshape(bsz, ntok, dim)
            return out @ p_w.T + p_b
        return _fwd(x, q_w1, q_b1, q_w2, q_b2, k_w1, k_b1, k_w2, k_b2, v_w, v_b, g_w, g_b, p_w, p_b)

    def _L0_ffn_ref(hidden_states, router_weight, e_bias, gate_w, up_w, down_w, sh_gate_w, sh_up_w, sh_down_w):
        import jax, jax.numpy as jnp
        import numpy as np
        B, S, H = (1, 512, 256)
        E, K = (16, 4)
        G, TG = (4, 2)
        I_MOE = 128
        N_SH = 2
        SCALE = 2.5

        def _mlp(x, gw, uw, dw):
            return jax.nn.silu(x @ gw.T) * (x @ uw.T) @ dw.T

        def _route(x2d, router_weight, e_bias):
            T = x2d.shape[0]
            scores = jax.nn.sigmoid(x2d @ router_weight.T)
            sc = scores + e_bias[None, :]
            group_scores = jnp.sum(jax.lax.top_k(sc.reshape(T, G, E // G), 2)[0], axis=-1)
            _, gidx = jax.lax.top_k(group_scores, TG)
            gmask = jnp.zeros((T, G), sc.dtype).at[jnp.arange(T)[:, None], gidx].set(1.0)
            smask = jnp.repeat(gmask, E // G, axis=1)
            masked = jnp.where(smask > 0, sc, 0.0)
            _, tidx = jax.lax.top_k(masked, K)
            tw = jnp.take_along_axis(scores, tidx, axis=1)
            tw = tw / (jnp.sum(tw, axis=-1, keepdims=True) + 1e-20)
            tw = tw * SCALE
            return (tidx, tw)

        def _moe_forward(hidden_states, router_weight, e_bias, gate_w, up_w, down_w, sh_gate_w, sh_up_w, sh_down_w):
            orig_shape = hidden_states.shape
            x = hidden_states.reshape(-1, H)
            T = x.shape[0]
            tidx, tw = _route(x, router_weight, e_bias)
            g = jnp.einsum('th,eih->tei', x, gate_w)
            u = jnp.einsum('th,eih->tei', x, up_w)
            h = jax.nn.silu(g) * u
            yo = jnp.einsum('tei,ehi->teh', h, down_w)
            combine = jnp.zeros((T, E), tw.dtype).at[jnp.arange(T)[:, None], tidx].add(tw)
            routed = jnp.einsum('te,teh->th', combine, yo)
            shared = _mlp(hidden_states.reshape(-1, H), sh_gate_w, sh_up_w, sh_down_w)
            return (routed + shared).reshape(orig_shape)
        return _moe_forward(hidden_states, router_weight, e_bias, gate_w, up_w, down_w, sh_gate_w, sh_up_w, sh_down_w)
    x = L0_attn_x
    x = x + 0.5 * _L0_ffn_ref(_layernorm(x, axis=-1), L0_ffn_router_weight, L0_ffn_e_bias, L0_ffn_gate_w, L0_ffn_up_w, L0_ffn_down_w, L0_ffn_sh_gate_w, L0_ffn_sh_up_w, L0_ffn_sh_down_w)
    x = x + _L0_attn_ref(_layernorm(x, axis=-1), L0_attn_q_w1, L0_attn_q_b1, L0_attn_q_w2, L0_attn_q_b2, L0_attn_k_w1, L0_attn_k_b1, L0_attn_k_w2, L0_attn_k_b2, L0_attn_v_w, L0_attn_v_b, L0_attn_g_w, L0_attn_g_b, L0_attn_p_w, L0_attn_p_b)
    x = x + 0.5 * _L0_ffn_ref(_layernorm(x, axis=-1), L0_ffn_router_weight, L0_ffn_e_bias, L0_ffn_gate_w, L0_ffn_up_w, L0_ffn_down_w, L0_ffn_sh_gate_w, L0_ffn_sh_up_w, L0_ffn_sh_down_w)
    return x

_drawn_inputs = setup_inputs


def setup_inputs(seed=0):
    import zlib

    import numpy as np

    out = dict(_drawn_inputs(seed))
    spreads = {'L0_ffn_e_bias': (0.0, 0.48)}
    factors = {'L0_attn_q_w1': 8.0,
     'L0_attn_q_b1': 59.559,
     'L0_attn_q_w2': 8.0,
     'L0_attn_q_b2': 64.0,
     'L0_attn_k_w1': 8.0,
     'L0_attn_k_b1': 22.423,
     'L0_attn_k_w2': 8.0,
     'L0_attn_k_b2': 28.327,
     'L0_attn_v_w': 8.0,
     'L0_attn_v_b': 8.0,
     'L0_attn_g_w': 8.0,
     'L0_attn_g_b': 8.0,
     'L0_attn_p_w': 8.0,
     'L0_attn_p_b': 11.665,
     'L0_ffn_router_weight': 7.751,
     'L0_ffn_gate_w': 3.8,
     'L0_ffn_up_w': 3.746,
     'L0_ffn_down_w': 3.762,
     'L0_ffn_sh_gate_w': 3.383,
     'L0_ffn_sh_up_w': 3.346,
     'L0_ffn_sh_down_w': 3.347}
    for name, (base, spread) in spreads.items():
        noise = np.random.default_rng([zlib.crc32(name.encode()), seed]).standard_normal(out[name].shape)
        drawn = base * np.exp(spread * noise) if base else spread * noise
        out[name] = jnp.asarray(drawn.astype(out[name].dtype))
    for name, factor in factors.items():
        out[name] = (out[name] * factor).astype(out[name].dtype)
    return out
```

```python
from contextlib import ExitStack

import concourse.bass as bass
from concourse import mybir

ALU = mybir.AluOpType
ACT = mybir.ActivationFunctionType
F32 = mybir.dt.float32
F16 = mybir.dt.float16
AX_X = mybir.AxisListType.X

P = 128
SEQS, TOK, D = 16, 512, 256
TT = TOK // P
KT = D // P
HEADS, HD = 16, 16
ATT_SCALE = HD ** -0.5
E, TOPK, GROUPS, TOPG = 16, 4, 4, 2
EG = E // GROUPS
SHARED = 2
NE = E + SHARED
ROUTE_SCALE = 2.5
HALF = 0.5
LN_EPS = 1e-5
J16 = 16
Q32 = TOK // J16
W_SCALE = 64.0
INV_W = 1.0 / W_SCALE
SENTINEL = -1.0e38
MARK = 1.0e38
PADS = 8 - TOPK
DOWN_EV = 2 * (E + 1)
COMB_EV = TT * (E + 1)
RING = 6
SMALL = 16 * 9
ROUTE_STEPS = 22
CONSTS = 10
MIX_STEPS = 6
Q1, K1, V, G, Q2, K2 = range(6)


def macaron(nc, x, q_w1, q_b1, q_w2, q_b2, k_w1, k_b1, k_w2, k_b2, v_w, v_b, g_w, g_b, p_w, p_b,
            router_w, e_bias, gate_w, up_w, down_w, sh_gate_w, sh_up_w, sh_down_w, out):
    ctx = ExitStack()
    with ctx:
        def sb(name, shape, dt=F32):
            return ctx.enter_context(nc.sbuf_tensor(name, shape, dt))

        def sem(name):
            return ctx.enter_context(nc.semaphore(name))

        gu_hi = sb("gu_hi", [P, NE, 2, KT, P], F16)
        gu_lo = sb("gu_lo", [P, NE, 2, KT, P], F16)
        dn_hi = sb("dn_hi", [P, NE, D], F16)
        dn_lo = sb("dn_lo", [P, NE, D], F16)
        at_hi = sb("at_hi", [P, 6, KT, D], F16)
        at_lo = sb("at_lo", [P, 6, KT, D], F16)
        pw_hi = sb("pw_hi", [P, 4, D], F16)
        pw_lo = sb("pw_lo", [P, 4, D], F16)
        rt_hi = sb("rt_hi", [P, KT, E], F16)
        rt_lo = sb("rt_lo", [P, KT, E], F16)
        rstage = sb("rstage", [E, D])
        bstage = sb("bstage", [3 * KT, P])
        pgroup = sb("pgroup", [P, 2, 4, 2, 64])
        ident = sb("ident", [P, P])
        blockmask = sb("blockmask", [P, P])
        ones = sb("ones", [P, P])
        minus_half = sb("minus_half", [P, TT])
        ln_eps = sb("ln_eps", [P, TT])
        scratch = sb("scratch", [P, 2])
        before = sb("before", [P, GROUPS, GROUPS])
        after = sb("after", [P, GROUPS, GROUPS])
        bias_col = sb("bias_col", [P, 3, KT])
        row_bias = sb("row_bias", [P, 4, D])
        ebias = sb("ebias", [P, E])
        x0 = sb("x0", [P, TT, D])
        x1 = sb("x1", [P, TT, D])
        x1b = sb("x1b", [P, TT, D])
        x2 = sb("x2", [P, TT, D])
        xo = sb("xo", [P, TT, D])
        xn = sb("xn", [P, TT, D])
        xt_hi = {stage: sb(f"xt_hi_{stage}", [P, KT, TOK], F16) for stage in ("f1", "at", "f2")}
        xt_lo = {stage: sb(f"xt_lo_{stage}", [P, KT, TOK], F16) for stage in ("f1", "at", "f2")}
        bn = sb("bn", [P, TT, 6])
        mv = sb("mv", [P, TT, 2])
        veps = sb("veps", [P, TT])
        rstd = sb("rstd", [P, TT])
        silu_g = sb("silu_g", [P, 2, TOK])
        prod = sb("prod", [P, 2, TOK])
        h_hi = sb("h_hi", [P, 3, TOK], F16)
        h_lo = sb("h_lo", [P, 3, TOK], F16)
        scores = sb("scores", [P, TT, E])
        biased = sb("biased", [P, TT, E])
        pair_max = sb("pair_max", [P, TT * GROUPS, 2])
        pair_min = sb("pair_min", [P, TT * GROUPS, 2])
        first = sb("first", [P, TT * GROUPS])
        second_a = sb("second_a", [P, TT * GROUPS])
        second_b = sb("second_b", [P, TT * GROUPS])
        second = sb("second", [P, TT * GROUPS])
        gscore = sb("gscore", [P, TT, GROUPS])
        beats_ge = sb("beats_ge", [P, TT, GROUPS, GROUPS])
        beats_gt = sb("beats_gt", [P, TT, GROUPS, GROUPS])
        grank = sb("grank", [P, TT, GROUPS])
        gmask = sb("gmask", [P, TT, GROUPS])
        cand = sb("cand", [P, TT, E + PADS])
        top8 = sb("top8", [P, TT, 8])
        marked = sb("marked", [P, TT, E + PADS])
        chosen = sb("chosen", [P, TT, E])
        wsum = sb("wsum", [P, TT])
        wrec = sb("wrec", [P, TT])
        comb = {stage: sb(f"comb_{stage}", [P, TT, E]) for stage in ("f1", "f2")}
        act32 = sb("act32", [P, 3, KT, TOK])
        staging = act32[:].rearrange("p a k t -> p (a k) t")
        act_hi = sb("act_hi", [P, 3, KT, TOK], F16)
        act_lo = sb("act_lo", [P, 3, KT, TOK], F16)
        gate = sb("gate", [P, TT, D])
        kqx = sb("kqx", [P, 2, TT, D])
        soft_a = sb("soft_a", [P, TT * D])
        soft_b = sb("soft_b", [P, TT * D])
        kq_hi = sb("kq_hi", [P, 2, TT, D], F16)
        kq_lo = sb("kq_lo", [P, 2, TT, D], F16)
        kv = sb("kv", [P, 2, P])
        kvi = sb("kvi", [P, 2, P])
        zden = sb("zden", [P, 2, P])
        zrec = sb("zrec", [P, 2, P])
        mix = sb("mix", [P, 2, P])
        mix_hi = sb("mix_hi", [P, 2, P], F16)
        mix_lo = sb("mix_lo", [P, 2, P], F16)
        og = sb("og", [P, 8, 2, 4, HD])
        ot_hi = sb("ot_hi", [P, 4, 8, Q32], F16)
        ot_lo = sb("ot_lo", [P, 4, 8, Q32], F16)

        bank = [ctx.enter_context(nc.psum_tensor(f"bank{i}", [P, 512], F32)) for i in range(8)]
        gate_ps, up_ps = bank[0], bank[1]
        down_ps = [bank[2], bank[3]]
        side_ps = bank[4:8]

        w_loaded = [sem(f"w_loaded{i}") for i in range(RING)]
        small_loaded = sem("small_loaded")
        consts_ready = sem("consts_ready")
        w_turned = sem("w_turned")
        bias_turned = sem("bias_turned")
        w_hi_done = sem("w_hi_done")
        w_lo_done = sem("w_lo_done")
        p_grouped = sem("p_grouped")
        x_loaded = sem("x_loaded")
        stored = sem("stored")
        stats_done = sem("stats_done")
        veps_done = sem("veps_done")
        rstd_done = sem("rstd_done")
        xn_done = sem("xn_done")
        turned = sem("turned")
        xt_hi_done = sem("xt_hi_done")
        xt_lo_done = sem("xt_lo_done")
        logits_done = sem("logits_done")
        scores_done = sem("scores_done")
        route_step = sem("route_step")
        gate_done = sem("gate_done")
        up_done = sem("up_done")
        silu_done = sem("silu_done")
        prod_done = sem("prod_done")
        hi_done = sem("hi_done")
        lo_done = sem("lo_done")
        down_done = sem("down_done")
        comb_done = sem("comb_done")
        proj_done = sem("proj_done")
        gelu_done = sem("gelu_done")
        act_hi_done = sem("act_hi_done")
        act_lo_done = sem("act_lo_done")
        gproj_done = sem("gproj_done")
        gx_done = sem("gx_done")
        gate_ready = sem("gate_ready")
        kq2_done = sem("kq2_done")
        kqx_done = sem("kqx_done")
        soft_step = sem("soft_step")
        softplus_done = sem("softplus_done")
        kq_hi_done = sem("kq_hi_done")
        kq_lo_done = sem("kq_lo_done")
        x1b_done = sem("x1b_done")
        kq_sum_done = sem("kq_sum_done")
        kv_done = sem("kv_done")
        kv_masked = sem("kv_masked")
        z_done = sem("z_done")
        mix_step = sem("mix_step")
        apply_done = sem("apply_done")
        og_done = sem("og_done")
        regrouped = sem("regrouped")
        ot_hi_done = sem("ot_hi_done")
        ot_lo_done = sem("ot_lo_done")
        project_done = sem("project_done")
        x2_done = sem("x2_done")

        block = ctx.enter_context(nc.Block())

        groups = [("gu", e) for e in range(NE)] + [("dn", e) for e in range(0, NE, 2)]
        groups += [("at", a) for a in range(6)] + [("pw", 0), ("pw", 2)]
        NG = len(groups)
        at_src = {Q1: q_w1, K1: k_w1, V: v_w, G: g_w, Q2: q_w2, K2: k_w2}

        def weight_dmas(kind, i):
            if kind == "gu":
                if i < E:
                    return [((0, 256), gate_w[i]), ((256, 512), up_w[i])]
                row = (i - E) * P
                return [((0, 256), sh_gate_w[row:row + P, :]), ((256, 512), sh_up_w[row:row + P, :])]
            if kind == "dn":
                if i < E:
                    return [((0, 512), down_w[i:i + 2].rearrange("e (h p) i -> p e h i", p=P))]
                return [((256 * j, 256 * j + 256),
                         sh_down_w[:, j * P:(j + 1) * P].rearrange("(h p) i -> p h i", p=P)) for j in range(2)]
            if kind == "at":
                return [((0, 512), at_src[i].rearrange("(h p) i -> p h i", p=P))]
            return [((0, 512), p_w.rearrange("(h p) i -> p h i", p=P))] if i == 0 else []

        slot_use, loads_of = [0] * RING, []
        for n, (kind, i) in enumerate(groups):
            slot_use[n % RING] += 16 * len(weight_dmas(kind, i))
            loads_of.append(slot_use[n % RING])

        def blocks_of(n):
            kind, i = groups[n]
            st = staging[:, n % RING, :]
            if kind in ("gu", "dn"):
                return [st[:, b * P:(b + 1) * P] for b in range(4)]
            if kind == "at":
                return [st[:, h * 256 + k * P:h * 256 + (k + 1) * P] for k in range(KT) for h in range(2)]
            return [pgroup[:, h, j, :, :].rearrange("p c n -> p (c n)") for j in (i, i + 1) for h in range(2)]

        def resident(n):
            kind, i = groups[n]
            if kind == "gu":
                return [t[:, i].rearrange("p m k o -> p (m k o)") for t in (gu_hi, gu_lo)]
            if kind == "dn":
                return [t[:, i:i + 2].rearrange("p e o -> p (e o)") for t in (dn_hi, dn_lo)]
            if kind == "at":
                return [t[:, i].rearrange("p k o -> p (k o)") for t in (at_hi, at_lo)]
            return [t[:, i:i + 2].rearrange("p j o -> p (j o)") for t in (pw_hi, pw_lo)]

        def f2_call(s):
            return 2 * s - 2

        def f1_call(s):
            return 2 * s - 1

        xview = x.rearrange("s (t p) d -> s p t d", p=P)
        oview = out.rearrange("s (t p) d -> s p t d", p=P)
        xin = {"f1": x0, "at": x1, "f2": x2}
        xout = {"f1": x1, "f2": xo}

        def pipeline(fori, ffn, main, stats, norm, turn, route_a, route_b, kv_sum, kv_norm, apply, regroup, project):
            def attention_tail(n, piece):
                if piece == 1:
                    kv_sum(n)
                elif piece == 2:
                    kv_norm(n)
                elif piece == 3:
                    apply(n)
                elif piece == 4:
                    regroup(n)
                elif piece == 5:
                    project(n)

            def prologue(stage, n, p, routing, f, piece):
                if piece == 0:
                    stats(stage, p, n, f)
                elif piece == 1:
                    norm(stage, p)
                elif piece == 2:
                    turn(stage, p)
                elif piece == 3 and stage != "at":
                    route_a(stage, p, routing)
                elif piece == 4 and stage != "at":
                    route_b(stage, routing)

            def whole_prologue(stage, n, p, routing, f):
                for piece in range(5):
                    prologue(stage, n, p, routing, f, piece)

            def nothing(e):
                pass

            whole_prologue("f1", n=0, p=0, routing=0, f=None)
            ffn("f1", f=0, n=0, p=0, side=nothing)

            def beside_ffn1_of_1(e):
                attention_tail(0, e)
                prologue("f2", 0, 3, 2, None, e - 7)

            whole_prologue("at", n=0, p=1, routing=None, f=0)
            whole_prologue("f1", n=1, p=2, routing=1, f=None)
            main(n=0, f=0, p=1, last_p=2, routed=2)
            ffn("f1", f=1, n=1, p=2, side=beside_ffn1_of_1)

            with fori(2, SEQS) as s:
                def beside_ffn2(e):
                    prologue("at", s - 1, 3 * s - 2, None, 2 * s - 3, e - 1)
                    prologue("f1", s, 3 * s - 1, 2 * s - 1, None, e - 5)

                def beside_ffn1(e):
                    attention_tail(s - 1, e)
                    prologue("f2", s - 1, 3 * s, 2 * s, None, e - 7)

                ffn("f2", f=2 * s - 2, n=s - 2, p=3 * s - 3, side=beside_ffn2)
                main(n=s - 1, f=2 * s - 2, p=3 * s - 2, last_p=3 * s - 1, routed=2 * s)
                ffn("f1", f=2 * s - 1, n=s, p=3 * s - 1, side=beside_ffn1)

            last = SEQS - 1

            def beside_last_but_one_ffn2(e):
                prologue("at", last, 3 * last + 1, None, 2 * last - 1, e - 1)

            ffn("f2", f=2 * last, n=last - 1, p=3 * last, side=beside_last_but_one_ffn2)
            main(n=last, f=2 * last, p=3 * last + 1, last_p=3 * last + 1, routed=2 * last + 1)
            for piece in range(1, 6):
                attention_tail(last, piece)
            whole_prologue("f2", n=last, p=3 * last + 2, routing=2 * last + 1, f=None)
            ffn("f2", f=2 * last + 1, n=last, p=3 * last + 2, side=nothing)

        def known_zero(v):
            return isinstance(v, int) and v == 0

        @block.sync
        def _(sp):
            sp.dma_start(x0[:], xview[0]).then_inc(x_loaded, 16)
            for n, (kind, i) in enumerate(groups):
                if n >= RING:
                    sp.wait_ge(w_turned, n - RING + 1)
                for (a, b), src in weight_dmas(kind, i):
                    dst = staging[:, n % RING, a:b]
                    if len(src.shape) == 3:
                        dst = dst.rearrange("p (h i) -> p h i", h=src.shape[1])
                    if len(src.shape) == 4:
                        dst = dst.rearrange("p (e h i) -> p e h i", e=2, h=2)
                    sp.dma_start(dst, src).then_inc(w_loaded[n % RING], 16)

            def load_x(n, f):
                sp.wait_ge(comb_done, COMB_EV * f + TT)
                sp.dma_start(x0[:], xview[n]).then_inc(x_loaded, 16)

            def store_x(n, f):
                sp.wait_ge(comb_done, COMB_EV * (f + 1))
                sp.dma_start(oview[n], xo[:]).then_inc(stored, 16)

            load_x(1, 0)
            load_x(2, 1)
            with sp.Fori(2, SEQS - 1) as s:
                store_x(s - 2, f2_call(s))
                load_x(s + 1, f1_call(s))
            store_x(SEQS - 3, f2_call(SEQS - 1))
            store_x(SEQS - 2, f2_call(SEQS))
            store_x(SEQS - 1, 2 * SEQS - 1)
            sp.wait_ge(stored, 16 * SEQS)

        @block.tensor
        def _(pe):
            def three(out_ap, pairs):
                n = len(pairs)
                for i, (a_hi, a_lo, b_hi, b_lo) in enumerate(pairs):
                    pe.matmul(out_ap, a_hi, b_hi, start=(i == 0), stop=False)
                    pe.matmul(out_ap, a_hi, b_lo, start=False, stop=False)
                    last = pe.matmul(out_ap, a_lo, b_hi, start=False, stop=(i == n - 1))
                return last

            pe.wait_ge(consts_ready, 5)
            for n in range(NG):
                if groups[n][0] == "pw":
                    pe.wait_ge(p_grouped, 4)
                else:
                    pe.wait_ge(w_loaded[n % RING], loads_of[n])
                if n >= 4:
                    pe.wait_ge(w_lo_done, n - 3)
                for b, src in enumerate(blocks_of(n)):
                    last = pe.transpose(side_ps[n % 4][:, b * P:(b + 1) * P], src, ident[:])
                last.then_inc(w_turned, 1)
            pe.wait_ge(small_loaded, SMALL)
            pe.wait_ge(w_lo_done, NG)
            for k in range(KT):
                last = pe.transpose(side_ps[0][:, k * E:(k + 1) * E], rstage[:, k * P:(k + 1) * P], ident[0:E, 0:E])
            last = pe.transpose(side_ps[0][:, KT * E:KT * E + 3 * KT], bstage[:], ident[0:3 * KT, 0:3 * KT])
            last.then_inc(w_turned, 1)
            pe.wait_ge(w_lo_done, NG + 1)
            pe.wait_ge(bias_turned, 1)

            def nothing(*_):
                pass

            def turn(stage, p):
                pe.wait_ge(xn_done, p + 1)
                if not known_zero(p):
                    pe.wait_ge(xt_hi_done, 2 * p)
                    pe.wait_ge(xt_lo_done, 2 * p)
                for k in range(KT):
                    for t in range(TT):
                        last = pe.transpose(side_ps[k][:, t * P:(t + 1) * P], xn[:, t, k * P:(k + 1) * P], ident[:])
                    last.then_inc(turned, 1)

            def route_a(stage, p, routing):
                pe.wait_ge(xt_hi_done, 2 * p + 2)
                pe.wait_ge(xt_lo_done, 2 * p + 2)
                for t in range(TT):
                    c = slice(t * P, (t + 1) * P)
                    last = three(side_ps[2][:, t * E:(t + 1) * E],
                                 [(xt_hi[stage][:, k, c], xt_lo[stage][:, k, c], rt_hi[:, k, :], rt_lo[:, k, :]) for k in range(KT)])
                last.then_inc(logits_done, 1)

            def down(f, e):
                last_e = e if e < E else E + SHARED - 1
                pe.wait_ge(hi_done, NE * f + last_e + 1)
                pe.wait_ge(lo_done, NE * f + last_e + 1)
                for b in range(2):
                    if e > 0 or not known_zero(f):
                        pe.wait_ge(comb_done, COMB_EV * f + TT * (e - 1) + 2 * b + 2)
                    for t in (2 * b, 2 * b + 1):
                        c = slice(t * P, (t + 1) * P)
                        dst = down_ps[b][:, (t % 2) * D:(t % 2 + 1) * D]
                        h_h, h_l = h_hi[:, e % 3, c], h_lo[:, e % 3, c]
                        if e < E:
                            pe.matmul(dst, h_h, dn_hi[:, e, :], start=True, stop=False)
                            pe.matmul(dst, h_h, dn_lo[:, e, :], start=False, stop=False)
                            last = pe.matmul(dst, h_l, dn_hi[:, e, :], start=False, stop=True)
                        else:
                            for i, j in enumerate((E, E + 1)):
                                a_h, a_l = h_hi[:, j % 3, c], h_lo[:, j % 3, c]
                                pe.matmul(dst, a_h, dn_hi[:, j, :], start=(i == 0), stop=False)
                                pe.matmul(dst, a_h, dn_lo[:, j, :], start=False, stop=False)
                                last = pe.matmul(dst, a_l, dn_hi[:, j, :], start=False, stop=(i == 1))
                    last.then_inc(down_done, 1)

            def ffn(stage, f, n, p, side):
                pe.wait_ge(xt_hi_done, 2 * p + 2)
                pe.wait_ge(xt_lo_done, 2 * p + 2)
                if stage == "f1" and not known_zero(n):
                    pe.wait_ge(gelu_done, 6 * n)
                    pe.wait_ge(gx_done, 2 * n)
                for e in range(NE):
                    g = NE * f + e
                    if e > 0 or not known_zero(f):
                        pe.wait_ge(silu_done, g)
                    three(gate_ps[:], [(gu_hi[:, e, 0, k], gu_lo[:, e, 0, k], xt_hi[stage][:, k], xt_lo[stage][:, k])
                                       for k in range(KT)]).then_inc(gate_done, 1)
                    if e > 0 or not known_zero(f):
                        pe.wait_ge(prod_done, g)
                    three(up_ps[:], [(gu_hi[:, e, 1, k], gu_lo[:, e, 1, k], xt_hi[stage][:, k], xt_lo[stage][:, k])
                                     for k in range(KT)]).then_inc(up_done, 1)
                    if e >= 2:
                        down(f, e - 2)
                    side(e)
                down(f, E)

            def main(n, f, p, last_p, routed):
                hi, lo = xt_hi["at"], xt_lo["at"]
                pe.wait_ge(xt_lo_done, 2 * last_p + 2)
                pe.wait_ge(xt_hi_done, 2 * last_p + 2)
                pe.wait_ge(scores_done, routed)
                dst = [side_ps[0], side_ps[1], side_ps[2], side_ps[3], gate_ps, up_ps]
                for i, a in enumerate((K1, K1, Q1, Q1, V, V)):
                    h = i % 2
                    if i == 4:
                        pe.wait_ge(silu_done, NE * (f + 1))
                        pe.wait_ge(prod_done, NE * (f + 1))
                    three(dst[i][:], [(at_hi[:, a, k, h * P:(h + 1) * P], at_lo[:, a, k, h * P:(h + 1) * P],
                                       hi[:, k], lo[:, k]) for k in range(KT)]).then_inc(proj_done, 1)
                pe.wait_ge(comb_done, COMB_EV * (f + 1))
                for t in range(TT):
                    c = slice(t * P, (t + 1) * P)
                    last = three(down_ps[t // 2][:, (t % 2) * D:(t % 2 + 1) * D],
                                 [(hi[:, k, c], lo[:, k, c], at_hi[:, G, k], at_lo[:, G, k]) for k in range(KT)])
                    if t % 2:
                        last.then_inc(gproj_done, 1)
                for i, a in enumerate((K2, Q2)):
                    pe.wait_ge(act_lo_done, 6 * n + 2 * i + 2)
                    for t in range(TT):
                        c = slice(t * P, (t + 1) * P)
                        last = three(side_ps[2 * i + t // 2][:, (t % 2) * D:(t % 2 + 1) * D],
                                     [(act_hi[:, i, k, c], act_lo[:, i, k, c], at_hi[:, a, k], at_lo[:, a, k])
                                      for k in range(KT)])
                        if t % 2:
                            last.then_inc(kq2_done, 1)

            def kv_sum(n):
                pe.wait_ge(kq_lo_done, 2 * n + 2)
                for h in range(2):
                    c = slice(h * P, (h + 1) * P)
                    last = three(side_ps[0][:, h * P:(h + 1) * P],
                                 [(kq_hi[:, 0, t, c], kq_lo[:, 0, t, c], kq_hi[:, 1, t, c], kq_lo[:, 1, t, c])
                                  for t in range(TT)])
                last.then_inc(kv_done, 1)

            def kv_norm(n):
                pe.wait_ge(kv_masked, n + 1)
                pe.matmul(side_ps[1][:, 0:D], ones[:], kv[:].rearrange("p h m -> p (h m)"),
                          start=True, stop=True).then_inc(z_done, 1)

            def apply(n):
                pe.wait_ge(mix_step, MIX_STEPS * (n + 1))
                pe.wait_ge(act_lo_done, 6 * n + 6)
                for t in range(TT):
                    c = slice(t * P, (t + 1) * P)
                    for h in range(2):
                        last = three(side_ps[2 + t // 2][:, (t % 2) * D + h * P:(t % 2) * D + (h + 1) * P],
                                     [(act_hi[:, 2, h, c], act_lo[:, 2, h, c], mix_hi[:, h], mix_lo[:, h])])
                    if t % 2:
                        last.then_inc(apply_done, 1)

            def regroup(n):
                pe.wait_ge(og_done, TT * n + TT)
                for hh in range(8):
                    last = pe.transpose(side_ps[hh // 4][:, (hh % 4) * P:(hh % 4 + 1) * P],
                                        og[:, hh].rearrange("p h j n -> p (h j n)"), ident[:])
                    if hh % 4 == 3:
                        last.then_inc(regrouped, 1)

            def project(n):
                pe.wait_ge(ot_hi_done, 2 * n + 2)
                pe.wait_ge(ot_lo_done, 2 * n + 2)
                for gg in range(2):
                    for j in range(4):
                        for part in range(3):
                            for h in range(2):
                                rows = slice(64 * h, 64 * h + 64)
                                a = (ot_lo if part == 2 else ot_hi)[rows, j, 4 * gg:4 * gg + 4, :].rearrange("p h q -> p (h q)")
                                b = (pw_lo if part == 1 else pw_hi)[rows, j, :]
                                last = pe.matmul(side_ps[2 + h][:, gg * D:(gg + 1) * D], a, b,
                                                 start=(j == 0 and part == 0), stop=(j == 3 and part == 2))
                                if gg == 1 and j == 3 and part == 2:
                                    last.then_inc(project_done, 1)

            pipeline(pe.Fori, ffn=ffn, main=main, stats=nothing, norm=nothing, turn=turn, route_a=route_a, route_b=nothing,
                     kv_sum=kv_sum, kv_norm=kv_norm, apply=apply, regroup=regroup, project=project)

        @block.scalar
        def _(act):
            for i, (b, dst) in enumerate(((q_b1, 1), (k_b1, 0), (v_b, 2))):
                act.dma_start(bstage[dst * KT:(dst + 1) * KT, :], b.rearrange("(k p) -> k p", p=P)).then_inc(small_loaded, 16)
            for i, b in enumerate((g_b, k_b2, q_b2, p_b)):
                act.dma_start(row_bias[:, i, :], b.partition_broadcast(P)).then_inc(small_loaded, 16)
            act.dma_start(ebias[:], e_bias.partition_broadcast(P)).then_inc(small_loaded, 16)
            act.dma_start(rstage[:], router_w).then_inc(small_loaded, 16)
            for n in range(NG):
                act.wait_ge(w_turned, n + 1)
                act.activation(resident(n)[0], side_ps[n % 4][:], ACT.Copy, scale=W_SCALE).then_inc(w_hi_done, 1)
            act.wait_ge(w_turned, NG + 1)
            act.activation(rt_hi[:].rearrange("p k e -> p (k e)"), side_ps[0][:, 0:KT * E], ACT.Copy,
                           scale=W_SCALE).then_inc(w_hi_done, 1)
            act.activation(bias_col[:].rearrange("p b k -> p (b k)"), side_ps[0][:, KT * E:KT * E + 3 * KT],
                           ACT.Copy).then_inc(bias_turned, 1)
            act.wait_ge(bias_turned, 1)

            def nothing(*_):
                pass

            def turn(stage, p):
                for k in range(KT):
                    act.wait_ge(turned, 2 * p + k + 1)
                    src = side_ps[k][:]
                    dst = xt_hi[stage][:, k]
                    if stage == "at":
                        src = src.rearrange("p (q j) -> p j q", j=J16)
                        dst = dst.rearrange("p (j q) -> p j q", j=J16)
                    act.activation(dst, src, ACT.Copy).then_inc(xt_hi_done, 1)

            def route_a(stage, p, routing):
                act.wait_ge(logits_done, routing + 1)
                if not known_zero(routing):
                    act.wait_ge(route_step, ROUTE_STEPS * routing)
                act.activation(scores[:].rearrange("p t e -> p (t e)"), side_ps[2][:, 0:TT * E], ACT.Tanh,
                               scale=0.5 * INV_W).then_inc(scores_done, 1)

            def ffn(stage, f, n, p, side):
                for e in range(NE):
                    g = NE * f + e
                    act.wait_ge(gate_done, g + 1)
                    if e >= 2 or not known_zero(f):
                        act.wait_ge(prod_done, g - 1)
                    act.activation(silu_g[:, e % 2], gate_ps[:], ACT.Silu, scale=INV_W).then_inc(silu_done, 1)
                    act.wait_ge(prod_done, g + 1)
                    if e >= 3:
                        act.wait_ge(down_done, DOWN_EV * f + 2 * (e - 2))
                    elif not known_zero(f):
                        act.wait_ge(down_done, DOWN_EV * f - (2 if e == 0 else 0))
                    act.activation(h_hi[:, e % 3], prod[:, e % 2], ACT.Copy).then_inc(hi_done, 1)
                    side(e)

            def main(n, f, p, last_p, routed):
                src = [side_ps[0], side_ps[1], side_ps[2], side_ps[3], gate_ps, up_ps]
                for i in range(6):
                    act.wait_ge(proj_done, 6 * n + i + 1)
                    if not known_zero(n):
                        act.wait_ge(act_lo_done, 6 * n)
                    act.activation(act32[:, i // 2, i % 2], src[i][:], ACT.Gelu, scale=INV_W,
                                   bias=bias_col[:, i // 2, i % 2:i % 2 + 1]).then_inc(gelu_done, 1)
                for b in range(2):
                    act.wait_ge(gx_done, 2 * n + b + 1)
                    act.activation(gate[:, 2 * b:2 * b + 2], gate[:, 2 * b:2 * b + 2], ACT.Gelu).then_inc(gate_ready, 1)
                for i in range(2):
                    act.wait_ge(kqx_done, 4 * n + 2 * i + 2)
                    if i > 0 or not known_zero(n):
                        act.wait_ge(kq_hi_done, 2 * n + i)
                    act.activation(soft_a[:], kqx[:, i].rearrange("p t d -> p (t d)"), ACT.Abs).then_inc(soft_step, 1)
                    act.wait_ge(soft_step, 4 * n + 2 * i + 1)
                    act.activation(soft_b[:], soft_a[:], ACT.Exp, scale=-1.0).then_inc(soft_step, 1)
                    act.wait_ge(soft_step, 4 * n + 2 * i + 2)
                    act.activation(soft_a[:], soft_b[:], ACT.Ln, bias=1.0).then_inc(softplus_done, 1)

            def regroup(n):
                for b in range(2):
                    act.wait_ge(regrouped, 2 * n + b + 1)
                    act.activation(ot_hi[:, :, 4 * b:4 * b + 4, :].rearrange("p j h q -> p h j q"),
                                   side_ps[b][:].rearrange("p (h j q) -> p h j q", h=4, j=4),
                                   ACT.Copy).then_inc(ot_hi_done, 1)

            pipeline(act.Fori, ffn=ffn, main=main, stats=nothing, norm=nothing, turn=turn, route_a=route_a, route_b=nothing,
                     kv_sum=nothing, kv_norm=nothing, apply=nothing, regroup=regroup, project=nothing)
            act.wait_ge(stored, 16 * SEQS)

        @block.gpsimd
        def _(pool):
            pool.memset(ident[:], 0.0).then_inc(consts_ready, 1)
            pool.wait_ge(consts_ready, 1)
            pool.affine_select(out=ident[:], in_=ident[:], compare_op=ALU.not_equal, fill=1.0, base=0,
                               pattern=[[-1, P]], channel_multiplier=1).then_inc(consts_ready, 1)
            pool.memset(ones[:], 1.0).then_inc(consts_ready, 1)
            pool.wait_ge(consts_ready, 3)
            bm = blockmask[:].rearrange("p (b c) -> p b c", c=HD)
            on = ones[:].rearrange("p (b c) -> p b c", c=HD)
            pool.affine_select(out=bm, in_=on, compare_op=ALU.is_ge, fill=0.0, base=0,
                               pattern=[[-HD, P // HD], [0, HD]], channel_multiplier=1).then_inc(consts_ready, 1)
            pool.wait_ge(consts_ready, 4)
            pool.affine_select(out=bm, in_=bm, compare_op=ALU.is_ge, fill=0.0, base=HD - 1,
                               pattern=[[HD, P // HD], [0, HD]], channel_multiplier=-1).then_inc(consts_ready, 1)
            pool.memset(minus_half[:], -0.5).then_inc(consts_ready, 1)
            pool.memset(ln_eps[:], LN_EPS).then_inc(consts_ready, 1)
            one_g = ones[:, 0:GROUPS * GROUPS].rearrange("p (g j) -> p g j", j=GROUPS)
            pool.affine_select(out=before[:], in_=one_g, compare_op=ALU.is_ge, fill=0.0, base=-1,
                               pattern=[[1, GROUPS], [-1, GROUPS]], channel_multiplier=0).then_inc(consts_ready, 1)
            pool.affine_select(out=after[:], in_=one_g, compare_op=ALU.is_ge, fill=0.0, base=-1,
                               pattern=[[-1, GROUPS], [1, GROUPS]], channel_multiplier=0).then_inc(consts_ready, 1)
            pool.memset(cand[:], SENTINEL).then_inc(consts_ready, 1)
            pool.wait_ge(small_loaded, SMALL)
            pool.wait_ge(consts_ready, CONSTS)

            def nothing(*_):
                pass

            def stats(stage, p, n, f):
                pool.wait_ge(stats_done, 2 * p + 2)
                pool.tensor_tensor(veps[:], mv[:, :, 1], ln_eps[:], ALU.add).then_inc(veps_done, 1)
                pool.wait_ge(veps_done, p + 1)
                if not known_zero(p):
                    pool.wait_ge(xn_done, p)
                pool.tensor_tensor(rstd[:], veps[:], minus_half[:], ALU.pow).then_inc(rstd_done, 1)

            def ffn(stage, f, n, p, side):
                for e in range(NE):
                    g = NE * f + e
                    pool.wait_ge(hi_done, g + 1)
                    pool.tensor_tensor(h_lo[:, e % 3], prod[:, e % 2], h_hi[:, e % 3], ALU.subtract).then_inc(lo_done, 1)
                    side(e)

            def main(n, f, p, last_p, routed):
                pool.wait_ge(comb_done, COMB_EV * (f if not known_zero(n) else 1))
                if not known_zero(n):
                    pool.wait_ge(x2_done, 2 * n)
                pool.tensor_tensor(x1b[:], x1[:], row_bias[:, 3:4, :].broadcast_to([P, TT, D]),
                                   ALU.add).then_inc(x1b_done, 1)

            pipeline(pool.Fori, ffn=ffn, main=main, stats=stats, norm=nothing, turn=nothing, route_a=nothing, route_b=nothing,
                     kv_sum=nothing, kv_norm=nothing, apply=nothing, regroup=nothing, project=nothing)

        @block.vector
        def _(dve):
            def flat(ap):
                return ap.rearrange("p a b -> p (a b)")

            n_pw = groups.index(("pw", 0))
            dve.wait_ge(consts_ready, CONSTS)
            for n in range(NG):
                if n == n_pw:
                    dve.wait_ge(w_loaded[n % RING], loads_of[n])
                    for h in range(2):
                        src = staging[:, n % RING, h * 256:(h + 1) * 256].rearrange("p (J j n) -> p j J n", J=4, j=4)
                        for c in range(2):
                            dve.tensor_copy(pgroup[:, h, :, c, :].rearrange("p j (J n) -> p j J n", J=4),
                                            src).then_inc(p_grouped, 1)
                dve.wait_ge(w_hi_done, n + 1)
                hi, lo = resident(n)
                dve.scalar_tensor_tensor(out=lo, in0=side_ps[n % 4][:], scalar=W_SCALE, in1=hi,
                                         op0=ALU.mult, op1=ALU.subtract).then_inc(w_lo_done, 1)
            dve.wait_ge(w_hi_done, NG + 1)
            dve.wait_ge(bias_turned, 1)
            dve.scalar_tensor_tensor(out=flat(rt_lo[:]), in0=side_ps[0][:, 0:KT * E], scalar=W_SCALE, in1=flat(rt_hi[:]),
                                     op0=ALU.mult, op1=ALU.subtract).then_inc(w_lo_done, 1)
            dve.wait_ge(small_loaded, SMALL)

            def stats(stage, p, n, f):
                src = xin[stage]
                if stage == "f1":
                    dve.wait_ge(x_loaded, 16 * (n + 1))
                elif stage == "at":
                    dve.wait_ge(comb_done, COMB_EV * (f + 1))
                else:
                    dve.wait_ge(x2_done, 2 * (n + 1))
                for t in range(TT):
                    ins = dve.bn_stats(bn[:, t, :], src[:, t, :])
                ins.then_inc(stats_done, 1)
                dve.wait_ge(stats_done, 2 * p + 1)
                dve.memset(scratch[:, 0:1], 0.0)
                for t in range(TT):
                    ins = dve.bn_aggr(mv[:, t, :], bn[:, t, :])
                ins.then_inc(stats_done, 1)

            def norm(stage, p):
                dve.wait_ge(rstd_done, p + 1)
                if not known_zero(p):
                    dve.wait_ge(turned, 2 * p)
                for t in range(TT):
                    ins = dve.tensor_scalar(xn[:, t, :], xin[stage][:, t, :], mv[:, t, 0:1], rstd[:, t:t + 1],
                                            ALU.subtract, ALU.mult)
                ins.then_inc(xn_done, 1)

            def turn(stage, p):
                for k in range(KT):
                    dve.wait_ge(xt_hi_done, 2 * p + k + 1)
                    src, hi, lo = side_ps[k][:], xt_hi[stage][:, k], xt_lo[stage][:, k]
                    if stage == "at":
                        src = src.rearrange("p (q j) -> p j q", j=J16)
                        hi, lo = (a.rearrange("p (j q) -> p j q", j=J16) for a in (hi, lo))
                    dve.tensor_tensor(lo, src, hi, ALU.subtract).then_inc(xt_lo_done, 1)

            def route_link(routing, k, ins):
                ins.then_inc(route_step, 1)
                dve.wait_ge(route_step, ROUTE_STEPS * routing + k)

            def route_a(stage, p, routing):
                dve.wait_ge(scores_done, routing + 1)
                route_link(routing, 1, dve.tensor_scalar(flat(scores[:]), flat(scores[:]), 0.5, 0.5, ALU.mult, ALU.add))
                route_link(routing, 2, dve.tensor_tensor(biased[:], scores[:], ebias[:].unsqueeze(1).broadcast_to([P, TT, E]), ALU.add))
                by_group = flat(biased[:]).rearrange("p (g e) -> p g e", e=EG)
                dve.tensor_tensor(pair_max[:], by_group[:, :, 0:2], by_group[:, :, 2:4], ALU.max)
                route_link(routing, 3, dve.tensor_tensor(pair_min[:], by_group[:, :, 0:2], by_group[:, :, 2:4], ALU.min))
                dve.tensor_tensor(first[:], pair_max[:, :, 0], pair_max[:, :, 1], ALU.max)
                dve.tensor_tensor(second_a[:], pair_max[:, :, 0], pair_max[:, :, 1], ALU.min)
                route_link(routing, 4, dve.tensor_tensor(second_b[:], pair_min[:, :, 0], pair_min[:, :, 1], ALU.max))
                route_link(routing, 5, dve.tensor_tensor(second[:], second_a[:], second_b[:], ALU.max))
                route_link(routing, 6, dve.tensor_tensor(flat(gscore[:]), first[:], second[:], ALU.add))
                other = gscore[:].unsqueeze(2).broadcast_to([P, TT, GROUPS, GROUPS])
                own = gscore[:].unsqueeze(3).broadcast_to([P, TT, GROUPS, GROUPS])
                dve.tensor_tensor(beats_ge[:], other, own, ALU.is_ge)
                route_link(routing, 7, dve.tensor_tensor(beats_gt[:], other, own, ALU.is_gt))
                dve.tensor_tensor(beats_ge[:], beats_ge[:], before[:].unsqueeze(1).broadcast_to([P, TT, GROUPS, GROUPS]), ALU.mult)
                route_link(routing, 8, dve.tensor_tensor(beats_gt[:], beats_gt[:],
                                                   after[:].unsqueeze(1).broadcast_to([P, TT, GROUPS, GROUPS]), ALU.mult))
                route_link(routing, 9, dve.tensor_tensor(beats_ge[:], beats_ge[:], beats_gt[:], ALU.add))
                route_link(routing, 10, dve.tensor_reduce(grank[:], beats_ge[:], AX_X, ALU.add))
                route_link(routing, 11, dve.tensor_scalar(flat(gmask[:]), flat(grank[:]), float(TOPG), None, ALU.is_lt))
                route_link(routing, 12, dve.tensor_tensor(
                    cand[:, :, 0:E].rearrange("p t (g e) -> p t g e", e=EG), biased[:].rearrange("p t (g e) -> p t g e", e=EG),
                    gmask[:].unsqueeze(3).broadcast_to([P, TT, GROUPS, EG]), ALU.mult))

            def route_b(stage, routing):
                for t in range(TT):
                    ins = dve.max(top8[:, t, :], cand[:, t, :])
                route_link(routing, 13, ins)
                route_link(routing, 14, dve.memset(top8[:, :, TOPK:8], SENTINEL))
                dve.memset(scratch[:, 1:2], 0.0)
                for t in range(TT):
                    ins = dve.match_replace(out=marked[:, t, :], in_to_replace=top8[:, t, :], in_values=cand[:, t, :],
                                            imm_value=MARK)
                route_link(routing, 15, ins)
                route_link(routing, 16, dve.tensor_scalar(chosen[:], marked[:, :, 0:E], MARK, None, ALU.is_equal))
                route_link(routing, 17, dve.tensor_tensor(chosen[:], chosen[:], scores[:], ALU.mult))
                route_link(routing, 18, dve.tensor_reduce(wsum[:], chosen[:], AX_X, ALU.add))
                route_link(routing, 19, dve.tensor_scalar(wsum[:], wsum[:], 1e-20, None, ALU.add))
                route_link(routing, 20, dve.reciprocal(wrec[:], wsum[:]))
                route_link(routing, 21, dve.tensor_tensor(chosen[:], chosen[:], wrec[:].unsqueeze(2).broadcast_to([P, TT, E]), ALU.mult))
                route_link(routing, 22, dve.tensor_scalar(comb[stage][:], chosen[:], ROUTE_SCALE * HALF * INV_W, None, ALU.mult))

            def combine(stage, f, e):
                src, dst = (xin[stage] if e == 0 else xout[stage]), xout[stage]
                for t in range(TT):
                    if t % 2 == 0:
                        dve.wait_ge(down_done, DOWN_EV * f + 2 * e + t // 2 + 1)
                    if e > 0:
                        dve.wait_ge(comb_done, COMB_EV * f + TT * (e - 1) + t + 1)
                    weight = comb[stage][:, t, e:e + 1] if e < E else HALF * INV_W
                    dve.scalar_tensor_tensor(out=dst[:, t, :], in0=down_ps[t // 2][:, (t % 2) * D:(t % 2 + 1) * D],
                                             scalar=weight, in1=src[:, t, :], op0=ALU.mult,
                                             op1=ALU.add).then_inc(comb_done, 1)

            def ffn(stage, f, n, p, side):
                for e in range(NE):
                    g = NE * f + e
                    dve.wait_ge(up_done, g + 1)
                    dve.wait_ge(silu_done, g + 1)
                    if e >= 2 or not known_zero(f):
                        dve.wait_ge(lo_done, g - 1)
                    dve.scalar_tensor_tensor(out=prod[:, e % 2], in0=up_ps[:], scalar=INV_W, in1=silu_g[:, e % 2],
                                             op0=ALU.mult, op1=ALU.mult).then_inc(prod_done, 1)
                    if e == 2:
                        if stage == "f1" and not known_zero(n):
                            dve.wait_ge(x1b_done, n)
                        if stage == "f2" and not known_zero(n):
                            dve.wait_ge(stored, 16 * n)
                    if e >= 2:
                        combine(stage, f, e - 2)
                    side(e)
                combine(stage, f, E)

            def main(n, f, p, last_p, routed):
                if not known_zero(n):
                    dve.wait_ge(project_done, 2 * n)
                def split(i):
                    dve.wait_ge(gelu_done, 6 * n + i + 1)
                    a, h = i // 2, i % 2
                    dve.tensor_copy(act_hi[:, a, h], act32[:, a, h]).then_inc(act_hi_done, 1)
                    dve.wait_ge(act_hi_done, 6 * n + i + 1)
                    dve.tensor_tensor(act_lo[:, a, h], act32[:, a, h], act_hi[:, a, h], ALU.subtract).then_inc(act_lo_done, 1)

                def add_bias(src, dst, bias, done):
                    dve.scalar_tensor_tensor(out=dst, in0=src[:].rearrange("p (t d) -> p t d", d=D), scalar=INV_W,
                                             in1=row_bias[:, bias:bias + 1, :].broadcast_to([P, 2, D]),
                                             op0=ALU.mult, op1=ALU.add).then_inc(done, 1)

                for i in range(6):
                    split(i)
                for b in range(2):
                    dve.wait_ge(gproj_done, 2 * n + b + 1)
                    add_bias(down_ps[b], gate[:, 2 * b:2 * b + 2], 0, gx_done)
                for i in range(2):
                    for b in range(2):
                        dve.wait_ge(kq2_done, 4 * n + 2 * i + b + 1)
                        add_bias(side_ps[2 * i + b], kqx[:, i, 2 * b:2 * b + 2], 1 + i, kqx_done)
                for i in range(2):
                    dve.wait_ge(softplus_done, 2 * n + i + 1)
                    v = flat(kqx[:, i])
                    dve.scalar_tensor_tensor(out=v, in0=v, scalar=0.0, in1=soft_a[:], op0=ALU.max,
                                             op1=ALU.add).then_inc(kq_sum_done, 1)
                    dve.wait_ge(kq_sum_done, 2 * n + i + 1)
                    dve.tensor_copy(flat(kq_hi[:, i]), v).then_inc(kq_hi_done, 1)
                    dve.wait_ge(kq_hi_done, 2 * n + i + 1)
                    dve.tensor_tensor(flat(kq_lo[:, i]), v, flat(kq_hi[:, i]), ALU.subtract).then_inc(kq_lo_done, 1)

            def kv_sum(n):
                dve.wait_ge(kv_done, n + 1)
                dve.tensor_tensor(kv[:], side_ps[0][:, 0:D].rearrange("p (h m) -> p h m", h=2),
                                  blockmask[:].unsqueeze(1).broadcast_to([P, 2, P]), ALU.mult).then_inc(kv_masked, 1)

            def kv_norm(n):
                def link(k, ins):
                    ins.then_inc(mix_step, 1)
                    dve.wait_ge(mix_step, MIX_STEPS * n + k)
                dve.wait_ge(z_done, n + 1)
                dve.tensor_scalar(flat(zden[:]), side_ps[1][:, 0:D], ATT_SCALE, float(D), ALU.mult, ALU.add).then_inc(mix_step, 1)
                link(2, dve.scalar_tensor_tensor(out=kvi[:], in0=kv[:], scalar=ATT_SCALE,
                                                 in1=ident[:].unsqueeze(1).broadcast_to([P, 2, P]), op0=ALU.mult, op1=ALU.add))
                link(3, dve.reciprocal(zrec[:], zden[:]))
                link(4, dve.tensor_tensor(mix[:], kvi[:], zrec[:], ALU.mult))
                link(5, dve.tensor_copy(mix_hi[:], mix[:]))
                link(6, dve.tensor_tensor(mix_lo[:], mix[:], mix_hi[:], ALU.subtract))

            def apply(n):
                dve.wait_ge(gate_ready, 2 * n + 2)
                for t in range(TT):
                    dve.wait_ge(apply_done, 2 * n + t // 2 + 1)
                    dve.tensor_tensor(og[:, :, :, t, :].rearrange("p a h n -> p h a n"),
                                      down_view(side_ps[2 + t // 2], t), down_view(gate[:, t, :], None),
                                      ALU.mult).then_inc(og_done, 1)

            def down_view(ap, t):
                if t is not None:
                    ap = ap[:, (t % 2) * D:(t % 2 + 1) * D]
                return ap.rearrange("p (h a n) -> p h a n", h=2, n=HD)

            def regroup(n):
                for b in range(2):
                    dve.wait_ge(ot_hi_done, 2 * n + b + 1)
                    dve.tensor_tensor(ot_lo[:, :, 4 * b:4 * b + 4, :].rearrange("p j h q -> p h j q"),
                                      side_ps[b][:].rearrange("p (h j q) -> p h j q", h=4, j=4),
                                      ot_hi[:, :, 4 * b:4 * b + 4, :].rearrange("p j h q -> p h j q"),
                                      ALU.subtract).then_inc(ot_lo_done, 1)

            def project(n):
                dve.wait_ge(x1b_done, n + 1)
                dve.wait_ge(project_done, 2 * n + 2)
                for h in range(2):
                    dve.scalar_tensor_tensor(out=flat(x2[:, 2 * h:2 * h + 2]), in0=side_ps[2 + h][:], scalar=INV_W,
                                             in1=flat(x1b[:, 2 * h:2 * h + 2]), op0=ALU.mult, op1=ALU.add).then_inc(x2_done, 1)

            pipeline(dve.Fori, ffn=ffn, main=main, stats=stats, norm=norm, turn=turn, route_a=route_a, route_b=route_b,
                     kv_sum=kv_sum, kv_norm=kv_norm, apply=apply, regroup=regroup, project=project)


_INS = ["attn_x", "attn_q_w1", "attn_q_b1", "attn_q_w2", "attn_q_b2", "attn_k_w1", "attn_k_b1", "attn_k_w2",
        "attn_k_b2", "attn_v_w", "attn_v_b", "attn_g_w", "attn_g_b", "attn_p_w", "attn_p_b", "ffn_router_weight",
        "ffn_e_bias", "ffn_gate_w", "ffn_up_w", "ffn_down_w", "ffn_sh_gate_w", "ffn_sh_up_w", "ffn_sh_down_w"]


def kernel(**inputs):
    import numpy as _np
    import concourse.bacc as _bacc
    from concourse import mybir as _mybir
    from concourse.bass_utils import run_bass_kernel_spmd as _run

    nc = _bacc.Bacc("TRN2", target_bir_lowering=False, num_devices=1)
    arrays, args = {}, []
    for name in _INS:
        a = _np.ascontiguousarray(inputs["L0_" + name])
        arrays[f"in_{name}_dram"] = a
        args.append(nc.dram_tensor(f"in_{name}_dram", a.shape, _mybir.dt.from_np(a.dtype), kind="ExternalInput").ap())
    args.append(nc.dram_tensor("out_dram", (SEQS, TOK, D), F32, kind="ExternalOutput").ap())
    macaron(nc, *args)
    ran = _run(nc, [arrays], core_ids=[0])
    return ran.results[0]["out_dram"]
```

```python
from contextlib import ExitStack

import concourse.bass as bass
from concourse import mybir

ALU = mybir.AluOpType
ACT = mybir.ActivationFunctionType
F32 = mybir.dt.float32
F16 = mybir.dt.float16
AX_X = mybir.AxisListType.X

P = 128
SEQS, TOK, D = 16, 512, 256
TT = TOK // P
KT = D // P
HEADS, HD = 16, 16
ATT_SCALE = HD ** -0.5
E, TOPK, GROUPS, TOPG = 16, 4, 4, 2
EG = E // GROUPS
SHARED = 2
NE = E + SHARED
ROUTE_SCALE = 2.5
HALF = 0.5
LN_EPS = 1e-5
J16 = 16
Q32 = TOK // J16
W_SCALE = 64.0
INV_W = 1.0 / W_SCALE
SENTINEL = -1.0e38
MARK = 1.0e38
PADS = 8 - TOPK
DOWN_EV = 2 * (E + 1)
COMB_EV = TT * (E + 1)
RING = 6
FIRST_GROUPS = 6
SMALL = 16 * 9
ROUTE_STEPS = 22
CONSTS = 10
MIX_STEPS = 6
Q1, K1, V, G, Q2, K2 = range(6)


def macaron(nc, x, q_w1, q_b1, q_w2, q_b2, k_w1, k_b1, k_w2, k_b2, v_w, v_b, g_w, g_b, p_w, p_b,
            router_w, e_bias, gate_w, up_w, down_w, sh_gate_w, sh_up_w, sh_down_w, out):
    ctx = ExitStack()
    with ctx:
        def sb(name, shape, dt=F32):
            return ctx.enter_context(nc.sbuf_tensor(name, shape, dt))

        def sem(name):
            return ctx.enter_context(nc.semaphore(name))

        gu_hi = sb("gu_hi", [P, NE, 2, KT, P], F16)
        gu_lo = sb("gu_lo", [P, NE, 2, KT, P], F16)
        dn_hi = sb("dn_hi", [P, NE, D], F16)
        dn_lo = sb("dn_lo", [P, NE, D], F16)
        at_hi = sb("at_hi", [P, 6, KT, D], F16)
        at_lo = sb("at_lo", [P, 6, KT, D], F16)
        pw_hi = sb("pw_hi", [P, 4, D], F16)
        pw_lo = sb("pw_lo", [P, 4, D], F16)
        rt_hi = sb("rt_hi", [P, KT, E], F16)
        rt_lo = sb("rt_lo", [P, KT, E], F16)
        rstage = sb("rstage", [E, D])
        bstage = sb("bstage", [3 * KT, P])
        pgroup = sb("pgroup", [P, 2, 4, 2, 64])
        ident = sb("ident", [P, P])
        blockmask = sb("blockmask", [P, P])
        ones = sb("ones", [P, P])
        minus_half = sb("minus_half", [P, TT])
        ln_eps = sb("ln_eps", [P, TT])
        scratch = sb("scratch", [P, 2])
        before = sb("before", [P, GROUPS, GROUPS])
        after = sb("after", [P, GROUPS, GROUPS])
        bias_col = sb("bias_col", [P, 3, KT])
        row_bias = sb("row_bias", [P, 4, D])
        ebias = sb("ebias", [P, E])
        x0 = sb("x0", [P, TT, D])
        x1 = sb("x1", [P, TT, D])
        x1b = sb("x1b", [P, TT, D])
        x2 = sb("x2", [P, TT, D])
        xo = sb("xo", [P, TT, D])
        xn = sb("xn", [P, TT, D])
        xt_hi = {stage: sb(f"xt_hi_{stage}", [P, KT, TOK], F16) for stage in ("f1", "at", "f2")}
        xt_lo = {stage: sb(f"xt_lo_{stage}", [P, KT, TOK], F16) for stage in ("f1", "at", "f2")}
        bn = sb("bn", [P, TT, 6])
        mv = sb("mv", [P, TT, 2])
        veps = sb("veps", [P, TT])
        rstd = sb("rstd", [P, TT])
        silu_g = sb("silu_g", [P, 2, TOK])
        prod = sb("prod", [P, 2, TOK])
        h_hi = sb("h_hi", [P, 3, TOK], F16)
        h_lo = sb("h_lo", [P, 3, TOK], F16)
        scores = sb("scores", [P, TT, E])
        biased = sb("biased", [P, TT, E])
        pair_max = sb("pair_max", [P, TT * GROUPS, 2])
        pair_min = sb("pair_min", [P, TT * GROUPS, 2])
        first = sb("first", [P, TT * GROUPS])
        second_a = sb("second_a", [P, TT * GROUPS])
        second_b = sb("second_b", [P, TT * GROUPS])
        second = sb("second", [P, TT * GROUPS])
        gscore = sb("gscore", [P, TT, GROUPS])
        beats_ge = sb("beats_ge", [P, TT, GROUPS, GROUPS])
        beats_gt = sb("beats_gt", [P, TT, GROUPS, GROUPS])
        grank = sb("grank", [P, TT, GROUPS])
        gmask = sb("gmask", [P, TT, GROUPS])
        cand = sb("cand", [P, TT, E + PADS])
        top8 = sb("top8", [P, TT, 8])
        marked = sb("marked", [P, TT, E + PADS])
        chosen = sb("chosen", [P, TT, E])
        wsum = sb("wsum", [P, TT])
        wrec = sb("wrec", [P, TT])
        comb = {stage: sb(f"comb_{stage}", [P, TT, E]) for stage in ("f1", "f2")}
        act32 = sb("act32", [P, 3, KT, TOK])
        staging = act32[:].rearrange("p a k t -> p (a k) t")
        act_hi = sb("act_hi", [P, 3, KT, TOK], F16)
        act_lo = sb("act_lo", [P, 3, KT, TOK], F16)
        gate = sb("gate", [P, TT, D])
        kqx = sb("kqx", [P, 2, TT, D])
        soft = sb("soft", [P, 2, TT * D])
        kq_hi = sb("kq_hi", [P, 2, TT, D], F16)
        kq_lo = sb("kq_lo", [P, 2, TT, D], F16)
        kv = sb("kv", [P, 2, P])
        kvi = sb("kvi", [P, 2, P])
        zden = sb("zden", [P, 2, P])
        zrec = sb("zrec", [P, 2, P])
        mix = sb("mix", [P, 2, P])
        mix_hi = sb("mix_hi", [P, 2, P], F16)
        mix_lo = sb("mix_lo", [P, 2, P], F16)
        og = sb("og", [P, 8, 2, 4, HD])
        ot_hi = sb("ot_hi", [P, 4, 8, Q32], F16)
        ot_lo = sb("ot_lo", [P, 4, 8, Q32], F16)

        bank = [ctx.enter_context(nc.psum_tensor(f"bank{i}", [P, 512], F32)) for i in range(8)]
        gate_ps, up_ps = bank[0], bank[1]
        down_ps = [bank[2], bank[3]]
        side_ps = bank[4:8]

        w_loaded = [sem(f"w_loaded{i}") for i in range(RING)]
        small_loaded = sem("small_loaded")
        consts_ready = sem("consts_ready")
        w_turned = sem("w_turned")
        rt_hi_done = sem("rt_hi_done")
        rt_lo_done = sem("rt_lo_done")
        bias_turned = sem("bias_turned")
        small_turned = sem("small_turned")
        w_hi_done = sem("w_hi_done")
        w_lo_done = sem("w_lo_done")
        p_grouped = sem("p_grouped")
        x_loaded = sem("x_loaded")
        stored = sem("stored")
        stats_done = sem("stats_done")
        veps_done = sem("veps_done")
        rstd_done = sem("rstd_done")
        xn_done = sem("xn_done")
        turned = sem("turned")
        xt_hi_done = sem("xt_hi_done")
        xt_lo_done = sem("xt_lo_done")
        logits_done = sem("logits_done")
        scores_done = sem("scores_done")
        route_step = sem("route_step")
        gate_done = sem("gate_done")
        up_done = sem("up_done")
        silu_done = sem("silu_done")
        prod_done = sem("prod_done")
        hi_done = sem("hi_done")
        lo_done = sem("lo_done")
        down_done = sem("down_done")
        comb_done = sem("comb_done")
        proj_done = sem("proj_done")
        gelu_done = sem("gelu_done")
        act_hi_done = sem("act_hi_done")
        act_lo_done = sem("act_lo_done")
        gproj_done = sem("gproj_done")
        gate_biased = sem("gate_biased")
        gate_ready = sem("gate_ready")
        kq2_done = sem("kq2_done")
        kq_biased = sem("kq_biased")
        abs_done = sem("abs_done")
        exp_done = sem("exp_done")
        softplus_done = sem("softplus_done")
        kq_hi_done = sem("kq_hi_done")
        kq_lo_done = sem("kq_lo_done")
        x1b_done = sem("x1b_done")
        kq_summed = sem("kq_summed")
        kv_done = sem("kv_done")
        kv_masked = sem("kv_masked")
        z_done = sem("z_done")
        mix_step = sem("mix_step")
        apply_done = sem("apply_done")
        og_done = sem("og_done")
        regrouped = sem("regrouped")
        ot_hi_done = sem("ot_hi_done")
        ot_lo_done = sem("ot_lo_done")
        project_done = sem("project_done")
        x2_done = sem("x2_done")

        block = ctx.enter_context(nc.Block())

        groups = [g for e in range(0, NE, 2) for g in (("gu", e), ("gu", e + 1), ("dn", e))]
        groups += [("at", a) for a in (K1, Q1, V, K2, Q2, G)] + [("pw", 0), ("pw", 2)]
        NG = len(groups)
        at_src = {Q1: q_w1, K1: k_w1, V: v_w, G: g_w, Q2: q_w2, K2: k_w2}

        def weight_dmas(kind, i):
            if kind == "gu":
                if i < E:
                    return [((0, 256), gate_w[i]), ((256, 512), up_w[i])]
                row = (i - E) * P
                return [((0, 256), sh_gate_w[row:row + P, :]), ((256, 512), sh_up_w[row:row + P, :])]
            if kind == "dn":
                if i < E:
                    return [((0, 512), down_w[i:i + 2].rearrange("e (h p) i -> p e h i", p=P))]
                return [((256 * j, 256 * j + 256),
                         sh_down_w[:, j * P:(j + 1) * P].rearrange("(h p) i -> p h i", p=P)) for j in range(2)]
            if kind == "at":
                return [((0, 512), at_src[i].rearrange("(h p) i -> p h i", p=P))]
            return [((0, 512), p_w.rearrange("(h p) i -> p h i", p=P))] if i == 0 else []

        slot_use, loads_of = [0] * RING, []
        for n, (kind, i) in enumerate(groups):
            slot_use[n % RING] += 16 * len(weight_dmas(kind, i))
            loads_of.append(slot_use[n % RING])

        def blocks_of(n):
            kind, i = groups[n]
            st = staging[:, n % RING, :]
            if kind in ("gu", "dn"):
                return [st[:, b * P:(b + 1) * P] for b in range(4)]
            if kind == "at":
                return [st[:, h * 256 + k * P:h * 256 + (k + 1) * P] for k in range(KT) for h in range(2)]
            return [pgroup[:, h, j, :, :].rearrange("p c n -> p (c n)") for j in (i, i + 1) for h in range(2)]

        def resident(n):
            kind, i = groups[n]
            if kind == "gu":
                return [t[:, i].rearrange("p m k o -> p (m k o)") for t in (gu_hi, gu_lo)]
            if kind == "dn":
                return [t[:, i:i + 2].rearrange("p e o -> p (e o)") for t in (dn_hi, dn_lo)]
            if kind == "at":
                return [t[:, i].rearrange("p k o -> p (k o)") for t in (at_hi, at_lo)]
            return [t[:, i:i + 2].rearrange("p j o -> p (j o)") for t in (pw_hi, pw_lo)]

        def f2_call(s):
            return 2 * s - 2

        def f1_call(s):
            return 2 * s - 1

        xview = x.rearrange("s (t p) d -> s p t d", p=P)
        oview = out.rearrange("s (t p) d -> s p t d", p=P)
        xin = {"f1": x0, "at": x1, "f2": x2}
        xout = {"f1": x1, "f2": xo}

        def pipeline(fori, pieces):
            def do(name, *args):
                if name in pieces:
                    pieces[name](*args)

            def in_slots(slots, e):
                for name, *args in slots.get(e, []):
                    do(name, *args)

            def beside_ffn2(n, f1, p, with_ffn1):
                slots = {0: [("stats", "at", p, n, f1)], 1: [("norm", "at", p), ("add_pb", n, f1)],
                         2: [("turn", "at", p, n), ("turn_hi", "at", p), ("turn_lo", "at", p)],
                         3: [("project_in", n, 0, p)],
                         4: [("project_in", n, 1, p), ("gelu", n, 0)],
                         5: [("project_in", n, 2, p), ("gelu", n, 1), ("split", n, 0)],
                         6: [("split", n, 1)],
                         7: [("second", n, 0), ("gelu", n, 2)],
                         8: [("second", n, 1), ("split", n, 2), ("add_bias", n, 0)],
                         9: [("add_bias", n, 1), ("absolute", n, 0)],
                         10: [("absolute", n, 1), ("project_gate", n, 0), ("softplus_exp", n)],
                         11: [("gate_bias", n, 0)],
                         12: [("project_gate", n, 1), ("softplus_ln", n), ("gate_bias", n, 1)],
                         14: [("finish_kq", n, 0)],
                         15: [("split_kq", n, 0), ("finish_kq", n, 1)],
                         16: [("split_kq", n, 1)]}
                if with_ffn1:
                    routing = 2 * n + 1
                    slots[4].append(("stats", "f1", p + 1, n + 1, None))
                    slots[6].append(("norm", "f1", p + 1))
                    slots[9] += [("turn", "f1", p + 1, n + 1), ("turn_hi", "f1", p + 1)]
                    slots[10].append(("turn_lo", "f1", p + 1))
                    slots[11] += [("logits", "f1", p + 1, n + 1, routing), ("sigmoid", routing)]
                    slots[12] += [("route_scores", routing), ("route_groups", routing)]
                    slots[13] = [("route_experts", routing)]
                    slots[17] = [("route_weights", "f1", routing)]
                return lambda e: in_slots(slots, e)

            def beside_ffn1(n, p, routing):
                slots = {0: [("kv_sum", n), ("gate_gelu", n)], 1: [("kv_norm", n)], 2: [("mix", n)],
                         3: [("apply", n, routing)], 4: [("gate_out", n)],
                         5: [("regroup", n)], 6: [("project_out", n)], 7: [("residual", n)],
                         8: [("stats", "f2", p, n, None)], 9: [("norm", "f2", p)],
                         10: [("turn", "f2", p, n), ("turn_hi", "f2", p), ("turn_lo", "f2", p)],
                         11: [("logits", "f2", p, n, routing)], 12: [("sigmoid", routing)],
                         13: [("route_scores", routing)], 14: [("route_groups", routing)],
                         15: [("route_experts", routing)], 17: [("route_weights", "f2", routing)]}
                return lambda e: in_slots(slots, e)

            def alone(slots):
                for e in range(NE):
                    slots(e)

            do("stats", "f1", 0, 0, None)
            do("norm", "f1", 0)
            do("turn", "f1", 0, 0)
            do("turn_hi", "f1", 0)
            do("turn_lo", "f1", 0)
            do("logits", "f1", 0, 0, 0)
            do("sigmoid", 0)
            do("weights", 0, FIRST_GROUPS)
            do("route_scores", 0)
            do("route_groups", 0)
            do("route_experts", 0)
            do("route_weights", "f1", 0)
            do("ffn", "f1", 0, 0, 0, None, lambda e: do("weights", FIRST_GROUPS + 2 * e, FIRST_GROUPS + 2 * e + 2))
            do("finish", "f1", 0)
            alone(beside_ffn2(n=0, f1=0, p=1, with_ffn1=True))
            do("ffn", "f1", 1, 1, 2, None, beside_ffn1(n=0, p=3, routing=2))
            with fori(2, SEQS) as s:
                do("ffn", "f2", 2 * s - 2, s - 2, 3 * s - 3, "f1",
                   beside_ffn2(n=s - 1, f1=2 * s - 3, p=3 * s - 2, with_ffn1=True))
                do("ffn", "f1", 2 * s - 1, s, 3 * s - 1, "f2", beside_ffn1(n=s - 1, p=3 * s, routing=2 * s))
            last = SEQS - 1
            do("ffn", "f2", 2 * last, last - 1, 3 * last, "f1",
               beside_ffn2(n=last, f1=2 * last - 1, p=3 * last + 1, with_ffn1=False))
            do("finish", "f2", 2 * last)
            alone(beside_ffn1(n=last, p=3 * last + 2, routing=2 * last + 1))
            do("ffn", "f2", 2 * last + 1, last, 3 * last + 2, None, lambda e: None)
            do("finish", "f2", 2 * last + 1)

        def turn_ps(stage, k):
            return side_ps[2 + k] if stage == "f1" else side_ps[k]

        def known_zero(v):
            return isinstance(v, int) and v == 0

        @block.sync
        def _(sp):
            sp.dma_start(x0[:], xview[0]).then_inc(x_loaded, 16)
            for n, (kind, i) in enumerate(groups):
                if n >= RING:
                    sp.wait_ge(w_turned, n - RING + 1)
                for (a, b), src in weight_dmas(kind, i):
                    dst = staging[:, n % RING, a:b]
                    if len(src.shape) == 3:
                        dst = dst.rearrange("p (h i) -> p h i", h=src.shape[1])
                    if len(src.shape) == 4:
                        dst = dst.rearrange("p (e h i) -> p e h i", e=2, h=2)
                    sp.dma_start(dst, src).then_inc(w_loaded[n % RING], 16)

            def load_x(n, f):
                sp.wait_ge(comb_done, COMB_EV * f + TT)
                sp.dma_start(x0[:], xview[n]).then_inc(x_loaded, 16)

            def store_x(n, f):
                sp.wait_ge(comb_done, COMB_EV * (f + 1))
                sp.dma_start(oview[n], xo[:]).then_inc(stored, 16)

            load_x(1, 0)
            load_x(2, 1)
            with sp.Fori(2, SEQS - 1) as s:
                store_x(s - 2, f2_call(s))
                load_x(s + 1, f1_call(s))
            store_x(SEQS - 3, f2_call(SEQS - 1))
            store_x(SEQS - 2, f2_call(SEQS))
            store_x(SEQS - 1, 2 * SEQS - 1)
            sp.wait_ge(stored, 16 * SEQS)

        @block.tensor
        def _(pe):
            def three(out_ap, pairs):
                n = len(pairs)
                for i, (a_hi, a_lo, b_hi, b_lo) in enumerate(pairs):
                    pe.matmul(out_ap, a_hi, b_hi, start=(i == 0), stop=False)
                    pe.matmul(out_ap, a_hi, b_lo, start=False, stop=False)
                    last = pe.matmul(out_ap, a_lo, b_hi, start=False, stop=(i == n - 1))
                return last

            def weights(first, stop):
                for n in range(first, min(stop, NG)):
                    if groups[n][0] == "pw":
                        pe.wait_ge(p_grouped, 4)
                    else:
                        pe.wait_ge(w_loaded[n % RING], loads_of[n])
                    if n < 4:
                        pe.wait_ge(scores_done, 1)
                    else:
                        pe.wait_ge(w_lo_done, n - 3)
                    for b, src in enumerate(blocks_of(n)):
                        last = pe.transpose(side_ps[n % 4][:, b * P:(b + 1) * P], src, ident[:])
                    last.then_inc(w_turned, 1)

            def turn(stage, p, n):
                pe.wait_ge(xn_done, p + 1)
                if not known_zero(p):
                    pe.wait_ge(xt_hi_done, 2 * p)
                    pe.wait_ge(xt_lo_done, 2 * p)
                if stage == "f1" and not known_zero(p):
                    pe.wait_ge(kq_biased, 4 * n - 2)
                for k in range(KT):
                    for t in range(TT):
                        last = pe.transpose(turn_ps(stage, k)[:, t * P:(t + 1) * P], xn[:, t, k * P:(k + 1) * P], ident[:])
                    last.then_inc(turned, 1)

            def logits(stage, p, n, routing):
                pe.wait_ge(xt_hi_done, 2 * p + 2)
                pe.wait_ge(xt_lo_done, 2 * p + 2)
                for t in range(TT):
                    c = slice(t * P, (t + 1) * P)
                    last = three(side_ps[2][:, t * E:(t + 1) * E],
                                 [(xt_hi[stage][:, k, c], xt_lo[stage][:, k, c], rt_hi[:, k, :], rt_lo[:, k, :])
                                  for k in range(KT)])
                last.then_inc(logits_done, 1)

            def down(f, e):
                last_e = e if e < E else E + SHARED - 1
                pe.wait_ge(hi_done, NE * f + last_e + 1)
                pe.wait_ge(lo_done, NE * f + last_e + 1)
                for b in range(2):
                    if e > 0 or not known_zero(f):
                        pe.wait_ge(comb_done, COMB_EV * f + TT * (e - 1) + 2 * b + 2)
                    for t in (2 * b, 2 * b + 1):
                        c = slice(t * P, (t + 1) * P)
                        dst = down_ps[b][:, (t % 2) * D:(t % 2 + 1) * D]
                        h_h, h_l = h_hi[:, e % 3, c], h_lo[:, e % 3, c]
                        if e < E:
                            pe.matmul(dst, h_h, dn_hi[:, e, :], start=True, stop=False)
                            pe.matmul(dst, h_h, dn_lo[:, e, :], start=False, stop=False)
                            last = pe.matmul(dst, h_l, dn_hi[:, e, :], start=False, stop=True)
                        else:
                            for i, j in enumerate((E, E + 1)):
                                a_h, a_l = h_hi[:, j % 3, c], h_lo[:, j % 3, c]
                                pe.matmul(dst, a_h, dn_hi[:, j, :], start=(i == 0), stop=False)
                                pe.matmul(dst, a_h, dn_lo[:, j, :], start=False, stop=False)
                                last = pe.matmul(dst, a_l, dn_hi[:, j, :], start=False, stop=(i == 1))
                    last.then_inc(down_done, 1)

            def ffn(stage, f, n, p, previous, side):
                pe.wait_ge(xt_hi_done, 2 * p + 2)
                pe.wait_ge(xt_lo_done, 2 * p + 2)
                for e in range(NE):
                    g = NE * f + e
                    if known_zero(f):
                        pe.wait_ge(w_lo_done, groups.index(("gu", e)) + 1)
                    if e > 0 or not known_zero(f):
                        pe.wait_ge(silu_done, g)
                    three(gate_ps[:], [(gu_hi[:, e, 0, k], gu_lo[:, e, 0, k], xt_hi[stage][:, k], xt_lo[stage][:, k])
                                       for k in range(KT)]).then_inc(gate_done, 1)
                    if e > 0 or not known_zero(f):
                        pe.wait_ge(prod_done, g)
                    three(up_ps[:], [(gu_hi[:, e, 1, k], gu_lo[:, e, 1, k], xt_hi[stage][:, k], xt_lo[stage][:, k])
                                     for k in range(KT)]).then_inc(up_done, 1)
                    if e == 0 and previous is not None:
                        down(f - 1, E)
                    if e >= 2:
                        down(f, e - 2)
                    side(e)

            def finish(stage, f):
                down(f, E)

            def project_in(n, i, p):
                if i == 0:
                    pe.wait_ge(xt_hi_done, 2 * p + 2)
                    pe.wait_ge(xt_lo_done, 2 * p + 2)
                    if known_zero(n):
                        pe.wait_ge(w_lo_done, NG)
                if i == 1:
                    pe.wait_ge(scores_done, 2 * n + 1)
                if i == 2:
                    pe.wait_ge(gelu_done, 6 * n + 2)
                for h in range(2):
                    o = slice(h * P, (h + 1) * P)
                    a = (K1, Q1, V)[i]
                    three(side_ps[(0, 2, 0)[i] + h][:],
                          [(at_hi[:, a, k, o], at_lo[:, a, k, o], xt_hi["at"][:, k], xt_lo["at"][:, k])
                           for k in range(KT)]).then_inc(proj_done, 1)

            def second(n, i):
                pe.wait_ge(act_lo_done, 6 * n + 2 * i + 2)
                pe.wait_ge(gelu_done, 6 * n + 2 * i + 4)
                for t in range(TT):
                    c = slice(t * P, (t + 1) * P)
                    last = three(side_ps[(2, 0)[i] + t // 2][:, (t % 2) * D:(t % 2 + 1) * D],
                                 [(act_hi[:, i, k, c], act_lo[:, i, k, c], at_hi[:, (K2, Q2)[i], k], at_lo[:, (K2, Q2)[i], k])
                                  for k in range(KT)])
                    if t % 2:
                        last.then_inc(kq2_done, 1)

            def project_gate(n, b):
                pe.wait_ge(kq_biased, 4 * n + 4)
                for t in (2 * b, 2 * b + 1):
                    c = slice(t * P, (t + 1) * P)
                    last = three(side_ps[b][:, (t % 2) * D:(t % 2 + 1) * D],
                                 [(xt_hi["at"][:, k, c], xt_lo["at"][:, k, c], at_hi[:, G, k], at_lo[:, G, k])
                                  for k in range(KT)])
                last.then_inc(gproj_done, 1)

            def kv_sum(n):
                pe.wait_ge(kq_lo_done, 2 * n + 2)
                pe.wait_ge(gate_biased, 2 * n + 2)
                for h in range(2):
                    c = slice(h * P, (h + 1) * P)
                    last = three(side_ps[0][:, h * P:(h + 1) * P],
                                 [(kq_hi[:, 0, t, c], kq_lo[:, 0, t, c], kq_hi[:, 1, t, c], kq_lo[:, 1, t, c])
                                  for t in range(TT)])
                last.then_inc(kv_done, 1)

            def kv_norm(n):
                pe.wait_ge(kv_masked, n + 1)
                pe.matmul(side_ps[1][:, 0:D], ones[:], kv[:].rearrange("p h m -> p (h m)"),
                          start=True, stop=True).then_inc(z_done, 1)

            def apply(n, routing):
                pe.wait_ge(mix_step, MIX_STEPS * (n + 1))
                pe.wait_ge(act_lo_done, 6 * n + 6)
                pe.wait_ge(scores_done, routing)
                for t in range(TT):
                    c = slice(t * P, (t + 1) * P)
                    for h in range(2):
                        last = three(side_ps[2 + t // 2][:, (t % 2) * D + h * P:(t % 2) * D + (h + 1) * P],
                                     [(act_hi[:, 2, h, c], act_lo[:, 2, h, c], mix_hi[:, h], mix_lo[:, h])])
                    if t % 2:
                        last.then_inc(apply_done, 1)

            def regroup(n):
                pe.wait_ge(og_done, TT * n + TT)
                for hh in range(8):
                    last = pe.transpose(side_ps[hh // 4][:, (hh % 4) * P:(hh % 4 + 1) * P],
                                        og[:, hh].rearrange("p h j n -> p (h j n)"), ident[:])
                    if hh % 4 == 3:
                        last.then_inc(regrouped, 1)

            def project_out(n):
                pe.wait_ge(ot_hi_done, 2 * n + 2)
                pe.wait_ge(ot_lo_done, 2 * n + 2)
                for gg in range(2):
                    for j in range(4):
                        for part in range(3):
                            for h in range(2):
                                rows = slice(64 * h, 64 * h + 64)
                                a = (ot_lo if part == 2 else ot_hi)[rows, j, 4 * gg:4 * gg + 4, :].rearrange("p h q -> p (h q)")
                                b = (pw_lo if part == 1 else pw_hi)[rows, j, :]
                                last = pe.matmul(side_ps[2 + h][:, gg * D:(gg + 1) * D], a, b,
                                                 start=(j == 0 and part == 0), stop=(j == 3 and part == 2))
                                if gg == 1 and j == 3 and part == 2:
                                    last.then_inc(project_done, 1)

            pe.wait_ge(consts_ready, CONSTS)
            pe.wait_ge(small_loaded, SMALL)
            for k in range(KT):
                pe.transpose(side_ps[3][:, k * E:(k + 1) * E], rstage[:, k * P:(k + 1) * P], ident[0:E, 0:E])
            pe.transpose(side_ps[3][:, KT * E:KT * E + 3 * KT], bstage[:],
                         ident[0:3 * KT, 0:3 * KT]).then_inc(small_turned, 1)
            pe.wait_ge(rt_lo_done, 1)
            pe.wait_ge(bias_turned, 1)
            pipeline(pe.Fori, dict(weights=weights, turn=turn, logits=logits, ffn=ffn, finish=finish,
                                   project_in=project_in, second=second, project_gate=project_gate, kv_sum=kv_sum,
                                   kv_norm=kv_norm, apply=apply, regroup=regroup, project_out=project_out))

        @block.scalar
        def _(act):
            for i, (b, dst) in enumerate(((q_b1, 1), (k_b1, 0), (v_b, 2))):
                act.dma_start(bstage[dst * KT:(dst + 1) * KT, :], b.rearrange("(k p) -> k p", p=P)).then_inc(small_loaded, 16)
            for i, b in enumerate((g_b, k_b2, q_b2, p_b)):
                act.dma_start(row_bias[:, i, :], b.partition_broadcast(P)).then_inc(small_loaded, 16)
            act.dma_start(ebias[:], e_bias.partition_broadcast(P)).then_inc(small_loaded, 16)
            act.dma_start(rstage[:], router_w).then_inc(small_loaded, 16)
            act.wait_ge(small_turned, 1)
            act.activation(rt_hi[:].rearrange("p k e -> p (k e)"), side_ps[3][:, 0:KT * E], ACT.Copy,
                           scale=W_SCALE).then_inc(rt_hi_done, 1)
            act.activation(bias_col[:].rearrange("p b k -> p (b k)"), side_ps[3][:, KT * E:KT * E + 3 * KT],
                           ACT.Copy).then_inc(bias_turned, 1)
            act.wait_ge(bias_turned, 1)

            def weights(first, stop):
                for n in range(first, min(stop, NG)):
                    act.wait_ge(w_turned, n + 1)
                    act.activation(resident(n)[0], side_ps[n % 4][:], ACT.Copy, scale=W_SCALE).then_inc(w_hi_done, 1)

            def turn_hi(stage, p):
                for k in range(KT):
                    act.wait_ge(turned, 2 * p + k + 1)
                    src = turn_ps(stage, k)[:]
                    dst = xt_hi[stage][:, k]
                    if stage == "at":
                        src = src.rearrange("p (q j) -> p j q", j=J16)
                        dst = dst.rearrange("p (j q) -> p j q", j=J16)
                    act.activation(dst, src, ACT.Copy).then_inc(xt_hi_done, 1)

            def sigmoid(routing):
                act.wait_ge(logits_done, routing + 1)
                if not known_zero(routing):
                    act.wait_ge(route_step, ROUTE_STEPS * routing)
                act.activation(scores[:].rearrange("p t e -> p (t e)"), side_ps[2][:, 0:TT * E], ACT.Tanh,
                               scale=0.5 * INV_W).then_inc(scores_done, 1)

            def ffn(stage, f, n, p, previous, side):
                for e in range(NE):
                    g = NE * f + e
                    act.wait_ge(gate_done, g + 1)
                    if e >= 2 or not known_zero(f):
                        act.wait_ge(prod_done, g - 1)
                    act.activation(silu_g[:, e % 2], gate_ps[:], ACT.Silu, scale=INV_W).then_inc(silu_done, 1)
                    act.wait_ge(prod_done, g + 1)
                    if e >= 3:
                        act.wait_ge(down_done, DOWN_EV * f + 2 * (e - 2))
                    elif not known_zero(f):
                        act.wait_ge(down_done, DOWN_EV * f - (2 if e == 0 else 0))
                    act.activation(h_hi[:, e % 3], prod[:, e % 2], ACT.Copy).then_inc(hi_done, 1)
                    side(e)

            def gelu(n, i):
                for h in range(2):
                    act.wait_ge(proj_done, 6 * n + 2 * i + h + 1)
                    if not known_zero(n):
                        act.wait_ge(act_lo_done, 6 * n)
                    act.activation(act32[:, i, h], side_ps[(0, 2, 0)[i] + h][:], ACT.Gelu, scale=INV_W,
                                   bias=bias_col[:, i, h:h + 1]).then_inc(gelu_done, 1)

            def absolute(n, i):
                act.wait_ge(kq_biased, 4 * n + 2 * i + 2)
                if not known_zero(n):
                    act.wait_ge(kq_summed, 2 * n)
                act.activation(soft[:, i], kqx[:, i].rearrange("p t d -> p (t d)"), ACT.Abs).then_inc(abs_done, 1)

            def softplus_exp(n):
                for i in range(2):
                    act.wait_ge(abs_done, 2 * n + i + 1)
                    act.activation(soft[:, i], soft[:, i], ACT.Exp, scale=-1.0).then_inc(exp_done, 1)

            def softplus_ln(n):
                for i in range(2):
                    act.wait_ge(exp_done, 2 * n + i + 1)
                    act.activation(soft[:, i], soft[:, i], ACT.Ln, bias=1.0).then_inc(softplus_done, 1)

            def split_kq(n, i):
                act.wait_ge(kq_summed, 2 * n + i + 1)
                if not known_zero(n):
                    act.wait_ge(kv_done, n)
                    act.wait_ge(kq_lo_done, 2 * n)
                act.activation(kq_hi[:, i], kqx[:, i], ACT.Copy).then_inc(kq_hi_done, 1)

            def gate_gelu(n):
                for b in range(2):
                    act.wait_ge(gate_biased, 2 * n + b + 1)
                    act.activation(gate[:, 2 * b:2 * b + 2], gate[:, 2 * b:2 * b + 2], ACT.Gelu).then_inc(gate_ready, 1)

            def regroup(n):
                for b in range(2):
                    act.wait_ge(regrouped, 2 * n + b + 1)
                    act.activation(ot_hi[:, :, 4 * b:4 * b + 4, :].rearrange("p j h q -> p h j q"),
                                   side_ps[b][:].rearrange("p (h j q) -> p h j q", h=4, j=4),
                                   ACT.Copy).then_inc(ot_hi_done, 1)

            pipeline(act.Fori, dict(weights=weights, turn_hi=turn_hi, sigmoid=sigmoid, ffn=ffn, gelu=gelu,
                                    absolute=absolute, split_kq=split_kq, softplus_exp=softplus_exp, softplus_ln=softplus_ln, gate_gelu=gate_gelu, regroup=regroup))
            act.wait_ge(stored, 16 * SEQS)

        @block.gpsimd
        def _(pool):
            pool.memset(ident[:], 0.0).then_inc(consts_ready, 1)
            pool.wait_ge(consts_ready, 1)
            pool.affine_select(out=ident[:], in_=ident[:], compare_op=ALU.not_equal, fill=1.0, base=0,
                               pattern=[[-1, P]], channel_multiplier=1).then_inc(consts_ready, 1)
            pool.memset(ones[:], 1.0).then_inc(consts_ready, 1)
            pool.wait_ge(consts_ready, 3)
            bm = blockmask[:].rearrange("p (b c) -> p b c", c=HD)
            on = ones[:].rearrange("p (b c) -> p b c", c=HD)
            pool.affine_select(out=bm, in_=on, compare_op=ALU.is_ge, fill=0.0, base=0,
                               pattern=[[-HD, P // HD], [0, HD]], channel_multiplier=1).then_inc(consts_ready, 1)
            pool.wait_ge(consts_ready, 4)
            pool.affine_select(out=bm, in_=bm, compare_op=ALU.is_ge, fill=0.0, base=HD - 1,
                               pattern=[[HD, P // HD], [0, HD]], channel_multiplier=-1).then_inc(consts_ready, 1)
            pool.memset(minus_half[:], -0.5).then_inc(consts_ready, 1)
            pool.memset(ln_eps[:], LN_EPS).then_inc(consts_ready, 1)
            one_g = ones[:, 0:GROUPS * GROUPS].rearrange("p (g j) -> p g j", j=GROUPS)
            pool.affine_select(out=before[:], in_=one_g, compare_op=ALU.is_ge, fill=0.0, base=-1,
                               pattern=[[1, GROUPS], [-1, GROUPS]], channel_multiplier=0).then_inc(consts_ready, 1)
            pool.affine_select(out=after[:], in_=one_g, compare_op=ALU.is_ge, fill=0.0, base=-1,
                               pattern=[[-1, GROUPS], [1, GROUPS]], channel_multiplier=0).then_inc(consts_ready, 1)
            pool.memset(cand[:], SENTINEL).then_inc(consts_ready, 1)
            pool.wait_ge(small_loaded, SMALL)
            pool.wait_ge(consts_ready, CONSTS)

            def stats(stage, p, n, f):
                pool.wait_ge(stats_done, 2 * p + 2)
                pool.tensor_tensor(veps[:], mv[:, :, 1], ln_eps[:], ALU.add).then_inc(veps_done, 1)
                pool.wait_ge(veps_done, p + 1)
                if not known_zero(p):
                    pool.wait_ge(xn_done, p)
                pool.tensor_tensor(rstd[:], veps[:], minus_half[:], ALU.pow).then_inc(rstd_done, 1)

            def ffn(stage, f, n, p, previous, side):
                for e in range(NE):
                    g = NE * f + e
                    pool.wait_ge(hi_done, g + 1)
                    pool.tensor_tensor(h_lo[:, e % 3], prod[:, e % 2], h_hi[:, e % 3], ALU.subtract).then_inc(lo_done, 1)
                    side(e)

            def add_pb(n, f1):
                pool.wait_ge(comb_done, COMB_EV * (f1 + 1))
                if not known_zero(n):
                    pool.wait_ge(x2_done, 2 * n)
                pool.tensor_tensor(x1b[:], x1[:], row_bias[:, 3:4, :].broadcast_to([P, TT, D]),
                                   ALU.add).then_inc(x1b_done, 1)

            def split(n, i):
                for h in range(2):
                    pool.wait_ge(act_hi_done, 6 * n + 2 * i + h + 1)
                    pool.tensor_tensor(act_lo[:, i, h], act32[:, i, h], act_hi[:, i, h],
                                       ALU.subtract).then_inc(act_lo_done, 1)

            def split_kq(n, i):
                pool.wait_ge(kq_hi_done, 2 * n + i + 1)
                pool.tensor_tensor(kq_lo[:, i], kqx[:, i], kq_hi[:, i], ALU.subtract).then_inc(kq_lo_done, 1)

            pipeline(pool.Fori, dict(stats=stats, ffn=ffn, add_pb=add_pb, split=split, split_kq=split_kq))

        @block.vector
        def _(dve):
            def flat(ap):
                return ap.rearrange("p a b -> p (a b)")

            n_pw = groups.index(("pw", 0))
            dve.wait_ge(consts_ready, CONSTS)
            dve.wait_ge(rt_hi_done, 1)
            dve.wait_ge(bias_turned, 1)
            dve.scalar_tensor_tensor(out=flat(rt_lo[:]), in0=side_ps[3][:, 0:KT * E], scalar=W_SCALE, in1=flat(rt_hi[:]),
                                     op0=ALU.mult, op1=ALU.subtract).then_inc(rt_lo_done, 1)
            dve.wait_ge(small_loaded, SMALL)

            def weights(first, stop):
                for n in range(first, min(stop, NG)):
                    dve.wait_ge(w_hi_done, n + 1)
                    hi, lo = resident(n)
                    dve.scalar_tensor_tensor(out=lo, in0=side_ps[n % 4][:], scalar=W_SCALE, in1=hi,
                                             op0=ALU.mult, op1=ALU.subtract).then_inc(w_lo_done, 1)
                    if n == n_pw - 1:
                        dve.wait_ge(w_loaded[n_pw % RING], loads_of[n_pw])
                        for h in range(2):
                            src = staging[:, n_pw % RING, h * 256:(h + 1) * 256].rearrange("p (J j n) -> p j J n", J=4, j=4)
                            for c in range(2):
                                dve.tensor_copy(pgroup[:, h, :, c, :].rearrange("p j (J n) -> p j J n", J=4),
                                                src).then_inc(p_grouped, 1)

            def stats(stage, p, n, f):
                src = xin[stage]
                if stage == "f1":
                    dve.wait_ge(x_loaded, 16 * (n + 1))
                elif stage == "at":
                    dve.wait_ge(comb_done, COMB_EV * (f + 1))
                else:
                    dve.wait_ge(x2_done, 2 * (n + 1))
                for t in range(TT):
                    ins = dve.bn_stats(bn[:, t, :], src[:, t, :])
                ins.then_inc(stats_done, 1)
                dve.wait_ge(stats_done, 2 * p + 1)
                dve.memset(scratch[:, 0:1], 0.0)
                for t in range(TT):
                    ins = dve.bn_aggr(mv[:, t, :], bn[:, t, :])
                ins.then_inc(stats_done, 1)

            def norm(stage, p):
                dve.wait_ge(rstd_done, p + 1)
                if not known_zero(p):
                    dve.wait_ge(turned, 2 * p)
                for t in range(TT):
                    ins = dve.tensor_scalar(xn[:, t, :], xin[stage][:, t, :], mv[:, t, 0:1], rstd[:, t:t + 1],
                                            ALU.subtract, ALU.mult)
                ins.then_inc(xn_done, 1)

            def turn_lo(stage, p):
                for k in range(KT):
                    dve.wait_ge(xt_hi_done, 2 * p + k + 1)
                    src, hi, lo = turn_ps(stage, k)[:], xt_hi[stage][:, k], xt_lo[stage][:, k]
                    if stage == "at":
                        src = src.rearrange("p (q j) -> p j q", j=J16)
                        hi, lo = (a.rearrange("p (j q) -> p j q", j=J16) for a in (hi, lo))
                    dve.tensor_tensor(lo, src, hi, ALU.subtract).then_inc(xt_lo_done, 1)

            def route_link(routing, k, ins):
                ins.then_inc(route_step, 1)
                dve.wait_ge(route_step, ROUTE_STEPS * routing + k)

            def route_scores(routing):
                dve.wait_ge(scores_done, routing + 1)
                route_link(routing, 1, dve.tensor_scalar(flat(scores[:]), flat(scores[:]), 0.5, 0.5, ALU.mult, ALU.add))
                route_link(routing, 2, dve.tensor_tensor(biased[:], scores[:], ebias[:].unsqueeze(1).broadcast_to([P, TT, E]), ALU.add))
                by_group = flat(biased[:]).rearrange("p (g e) -> p g e", e=EG)
                dve.tensor_tensor(pair_max[:], by_group[:, :, 0:2], by_group[:, :, 2:4], ALU.max)
                route_link(routing, 3, dve.tensor_tensor(pair_min[:], by_group[:, :, 0:2], by_group[:, :, 2:4], ALU.min))

            def route_groups(routing):
                dve.tensor_tensor(first[:], pair_max[:, :, 0], pair_max[:, :, 1], ALU.max)
                dve.tensor_tensor(second_a[:], pair_max[:, :, 0], pair_max[:, :, 1], ALU.min)
                route_link(routing, 4, dve.tensor_tensor(second_b[:], pair_min[:, :, 0], pair_min[:, :, 1], ALU.max))
                route_link(routing, 5, dve.tensor_tensor(second[:], second_a[:], second_b[:], ALU.max))
                route_link(routing, 6, dve.tensor_tensor(flat(gscore[:]), first[:], second[:], ALU.add))
                other = gscore[:].unsqueeze(2).broadcast_to([P, TT, GROUPS, GROUPS])
                own = gscore[:].unsqueeze(3).broadcast_to([P, TT, GROUPS, GROUPS])
                dve.tensor_tensor(beats_ge[:], other, own, ALU.is_ge)
                route_link(routing, 7, dve.tensor_tensor(beats_gt[:], other, own, ALU.is_gt))
                dve.tensor_tensor(beats_ge[:], beats_ge[:], before[:].unsqueeze(1).broadcast_to([P, TT, GROUPS, GROUPS]), ALU.mult)
                route_link(routing, 8, dve.tensor_tensor(beats_gt[:], beats_gt[:],
                                                   after[:].unsqueeze(1).broadcast_to([P, TT, GROUPS, GROUPS]), ALU.mult))
                route_link(routing, 9, dve.tensor_tensor(beats_ge[:], beats_ge[:], beats_gt[:], ALU.add))

            def route_experts(routing):
                route_link(routing, 10, dve.tensor_reduce(grank[:], beats_ge[:], AX_X, ALU.add))
                route_link(routing, 11, dve.tensor_scalar(flat(gmask[:]), flat(grank[:]), float(TOPG), None, ALU.is_lt))
                route_link(routing, 12, dve.tensor_tensor(
                    cand[:, :, 0:E].rearrange("p t (g e) -> p t g e", e=EG), biased[:].rearrange("p t (g e) -> p t g e", e=EG),
                    gmask[:].unsqueeze(3).broadcast_to([P, TT, GROUPS, EG]), ALU.mult))
                dve.memset(scratch[:, 1:2], 0.0)
                for t in range(TT):
                    ins = dve.max(top8[:, t, :], cand[:, t, :])
                route_link(routing, 13, ins)
                route_link(routing, 14, dve.memset(top8[:, :, TOPK:8], SENTINEL))
                dve.memset(scratch[:, 1:2], 0.0)
                for t in range(TT):
                    ins = dve.match_replace(out=marked[:, t, :], in_to_replace=top8[:, t, :], in_values=cand[:, t, :],
                                            imm_value=MARK)
                route_link(routing, 15, ins)

            def route_weights(stage, routing):
                route_link(routing, 16, dve.tensor_scalar(chosen[:], marked[:, :, 0:E], MARK, None, ALU.is_equal))
                route_link(routing, 17, dve.tensor_tensor(chosen[:], chosen[:], scores[:], ALU.mult))
                route_link(routing, 18, dve.tensor_reduce(wsum[:], chosen[:], AX_X, ALU.add))
                route_link(routing, 19, dve.tensor_scalar(wsum[:], wsum[:], 1e-20, None, ALU.add))
                route_link(routing, 20, dve.reciprocal(wrec[:], wsum[:]))
                route_link(routing, 21, dve.tensor_tensor(chosen[:], chosen[:], wrec[:].unsqueeze(2).broadcast_to([P, TT, E]), ALU.mult))
                route_link(routing, 22, dve.tensor_scalar(comb[stage][:], chosen[:], ROUTE_SCALE * HALF * INV_W, None, ALU.mult))

            def combine(stage, f, e):
                src, dst = (xin[stage] if e == 0 else xout[stage]), xout[stage]
                for t in range(TT):
                    if t % 2 == 0:
                        dve.wait_ge(down_done, DOWN_EV * f + 2 * e + t // 2 + 1)
                    if e > 0:
                        dve.wait_ge(comb_done, COMB_EV * f + TT * (e - 1) + t + 1)
                    weight = comb[stage][:, t, e:e + 1] if e < E else HALF * INV_W
                    dve.scalar_tensor_tensor(out=dst[:, t, :], in0=down_ps[t // 2][:, (t % 2) * D:(t % 2 + 1) * D],
                                             scalar=weight, in1=src[:, t, :], op0=ALU.mult,
                                             op1=ALU.add).then_inc(comb_done, 1)

            def ffn(stage, f, n, p, previous, side):
                for e in range(NE):
                    g = NE * f + e
                    dve.wait_ge(up_done, g + 1)
                    dve.wait_ge(silu_done, g + 1)
                    if e >= 2 or not known_zero(f):
                        dve.wait_ge(lo_done, g - 1)
                    dve.scalar_tensor_tensor(out=prod[:, e % 2], in0=up_ps[:], scalar=INV_W, in1=silu_g[:, e % 2],
                                             op0=ALU.mult, op1=ALU.mult).then_inc(prod_done, 1)
                    if e == 0 and previous is not None:
                        combine(previous, f - 1, E)
                    if e == 2:
                        if stage == "f1" and not known_zero(n):
                            dve.wait_ge(x1b_done, n)
                        if stage == "f2" and not known_zero(n):
                            dve.wait_ge(stored, 16 * n)
                    if e >= 2:
                        combine(stage, f, e - 2)
                    side(e)

            def finish(stage, f):
                combine(stage, f, E)

            def split(n, i):
                for h in range(2):
                    dve.wait_ge(gelu_done, 6 * n + 2 * i + h + 1)
                    if not known_zero(n):
                        dve.wait_ge(apply_done, 2 * n)
                        dve.wait_ge(act_lo_done, 6 * n)
                    dve.tensor_copy(act_hi[:, i, h], act32[:, i, h]).then_inc(act_hi_done, 1)

            def unscale(src, dst, bias, done):
                dve.scalar_tensor_tensor(out=dst, in0=src[:].rearrange("p (t d) -> p t d", d=D), scalar=INV_W,
                                         in1=row_bias[:, bias:bias + 1, :].broadcast_to([P, 2, D]),
                                         op0=ALU.mult, op1=ALU.add).then_inc(done, 1)

            def add_bias(n, i):
                for b in range(2):
                    dve.wait_ge(kq2_done, 4 * n + 2 * i + b + 1)
                    if not known_zero(n):
                        dve.wait_ge(kq_lo_done, 2 * n)
                    unscale(side_ps[(2, 0)[i] + b], kqx[:, i, 2 * b:2 * b + 2], 1 + i, kq_biased)

            def gate_bias(n, b):
                dve.wait_ge(gproj_done, 2 * n + b + 1)
                if not known_zero(n):
                    dve.wait_ge(og_done, TT * n)
                unscale(side_ps[b], gate[:, 2 * b:2 * b + 2], 0, gate_biased)

            def finish_kq(n, i):
                dve.wait_ge(softplus_done, 2 * n + i + 1)
                v = flat(kqx[:, i])
                dve.scalar_tensor_tensor(out=v, in0=v, scalar=0.0, in1=soft[:, i], op0=ALU.max,
                                         op1=ALU.add).then_inc(kq_summed, 1)

            def kv_sum(n):
                dve.wait_ge(kv_done, n + 1)
                dve.tensor_tensor(kv[:], side_ps[0][:, 0:D].rearrange("p (h m) -> p h m", h=2),
                                  blockmask[:].unsqueeze(1).broadcast_to([P, 2, P]), ALU.mult).then_inc(kv_masked, 1)

            def kv_norm(n):
                def link(k, ins):
                    ins.then_inc(mix_step, 1)
                    dve.wait_ge(mix_step, MIX_STEPS * n + k)
                dve.wait_ge(z_done, n + 1)
                dve.tensor_scalar(flat(zden[:]), side_ps[1][:, 0:D], ATT_SCALE, float(D), ALU.mult, ALU.add).then_inc(mix_step, 1)
                link(2, dve.scalar_tensor_tensor(out=kvi[:], in0=kv[:], scalar=ATT_SCALE,
                                                 in1=ident[:].unsqueeze(1).broadcast_to([P, 2, P]), op0=ALU.mult, op1=ALU.add))
                link(3, dve.reciprocal(zrec[:], zden[:]))

            def mix_in(n):
                def link(k, ins):
                    ins.then_inc(mix_step, 1)
                    dve.wait_ge(mix_step, MIX_STEPS * n + k)
                link(4, dve.tensor_tensor(mix[:], kvi[:], zrec[:], ALU.mult))
                link(5, dve.tensor_copy(mix_hi[:], mix[:]))
                link(6, dve.tensor_tensor(mix_lo[:], mix[:], mix_hi[:], ALU.subtract))

            def gate_out(n):
                dve.wait_ge(gate_ready, 2 * n + 2)
                for t in range(TT):
                    dve.wait_ge(apply_done, 2 * n + t // 2 + 1)
                    dve.tensor_tensor(og[:, :, :, t, :].rearrange("p a h n -> p h a n"),
                                      down_view(side_ps[2 + t // 2], t), down_view(gate[:, t, :], None),
                                      ALU.mult).then_inc(og_done, 1)

            def down_view(ap, t):
                if t is not None:
                    ap = ap[:, (t % 2) * D:(t % 2 + 1) * D]
                return ap.rearrange("p (h a n) -> p h a n", h=2, n=HD)

            def regroup(n):
                for b in range(2):
                    dve.wait_ge(ot_hi_done, 2 * n + b + 1)
                    dve.tensor_tensor(ot_lo[:, :, 4 * b:4 * b + 4, :].rearrange("p j h q -> p h j q"),
                                      side_ps[b][:].rearrange("p (h j q) -> p h j q", h=4, j=4),
                                      ot_hi[:, :, 4 * b:4 * b + 4, :].rearrange("p j h q -> p h j q"),
                                      ALU.subtract).then_inc(ot_lo_done, 1)

            def residual(n):
                dve.wait_ge(x1b_done, n + 1)
                dve.wait_ge(project_done, 2 * n + 2)
                for h in range(2):
                    dve.scalar_tensor_tensor(out=flat(x2[:, 2 * h:2 * h + 2]), in0=side_ps[2 + h][:], scalar=INV_W,
                                             in1=flat(x1b[:, 2 * h:2 * h + 2]), op0=ALU.mult, op1=ALU.add).then_inc(x2_done, 1)

            pipeline(dve.Fori, dict(weights=weights, stats=stats, norm=norm, turn_lo=turn_lo, route_scores=route_scores,
                                    route_groups=route_groups,
                                    route_experts=route_experts, route_weights=route_weights, ffn=ffn, finish=finish,
                                    split=split, add_bias=add_bias, gate_bias=gate_bias, finish_kq=finish_kq,
                                    kv_sum=kv_sum, kv_norm=kv_norm, mix=mix_in, gate_out=gate_out, regroup=regroup,
                                    residual=residual))


_INS = ["attn_x", "attn_q_w1", "attn_q_b1", "attn_q_w2", "attn_q_b2", "attn_k_w1", "attn_k_b1", "attn_k_w2",
        "attn_k_b2", "attn_v_w", "attn_v_b", "attn_g_w", "attn_g_b", "attn_p_w", "attn_p_b", "ffn_router_weight",
        "ffn_e_bias", "ffn_gate_w", "ffn_up_w", "ffn_down_w", "ffn_sh_gate_w", "ffn_sh_up_w", "ffn_sh_down_w"]


def kernel(**inputs):
    import numpy as _np
    import concourse.bacc as _bacc
    from concourse import mybir as _mybir
    from concourse.bass_utils import run_bass_kernel_spmd as _run

    nc = _bacc.Bacc("TRN2", target_bir_lowering=False, num_devices=1)
    arrays, args = {}, []
    for name in _INS:
        a = _np.ascontiguousarray(inputs["L0_" + name])
        arrays[f"in_{name}_dram"] = a
        args.append(nc.dram_tensor(f"in_{name}_dram", a.shape, _mybir.dt.from_np(a.dtype), kind="ExternalInput").ap())
    args.append(nc.dram_tensor("out_dram", (SEQS, TOK, D), F32, kind="ExternalOutput").ap())
    macaron(nc, *args)
    ran = _run(nc, [arrays], core_ids=[0])
    return ran.results[0]["out_dram"]
```

```python
from contextlib import ExitStack

import concourse.bass as bass
from concourse import mybir

ALU = mybir.AluOpType
ACT = mybir.ActivationFunctionType
F32 = mybir.dt.float32
F16 = mybir.dt.float16
AX_X = mybir.AxisListType.X

P = 128
SEQS, TOK, D = 16, 512, 256
TT = TOK // P
KT = D // P
HEADS, HD = 16, 16
ATT_SCALE = HD ** -0.5
E, TOPK, GROUPS, TOPG = 16, 4, 4, 2
EG = E // GROUPS
SHARED = 2
NE = E + SHARED
ROUTE_SCALE = 2.5
HALF = 0.5
LN_EPS = 1e-5
J16 = 16
Q32 = TOK // J16
W_SCALE = 64.0
INV_W = 1.0 / W_SCALE
SENTINEL = -1.0e38
MARK = 1.0e38
PADS = 8 - TOPK
DOWN_EV = 2 * (E + 1)
COMB_EV = TT * (E + 1)
RING = 6
FIRST_GROUPS = 4
SMALL = 16 * 5
ROWS = 16 * 4
ROUTE_STEPS = 22
CONSTS = 10
MIX_STEPS = 6
Q1, K1, V, G, Q2, K2 = range(6)


def macaron(nc, x, q_w1, q_b1, q_w2, q_b2, k_w1, k_b1, k_w2, k_b2, v_w, v_b, g_w, g_b, p_w, p_b,
            router_w, e_bias, gate_w, up_w, down_w, sh_gate_w, sh_up_w, sh_down_w, out):
    ctx = ExitStack()
    with ctx:
        def sb(name, shape, dt=F32):
            return ctx.enter_context(nc.sbuf_tensor(name, shape, dt))

        def sem(name):
            return ctx.enter_context(nc.semaphore(name))

        gu_hi = sb("gu_hi", [P, NE, 2, KT, P], F16)
        gu_lo = sb("gu_lo", [P, NE, 2, KT, P], F16)
        dn_hi = sb("dn_hi", [P, NE, D], F16)
        dn_lo = sb("dn_lo", [P, NE, D], F16)
        at_hi = sb("at_hi", [P, 6, KT, D], F16)
        at_lo = sb("at_lo", [P, 6, KT, D], F16)
        pw_hi = sb("pw_hi", [P, 2, D], F16)
        pw_lo = sb("pw_lo", [P, 2, D], F16)
        rt_hi = sb("rt_hi", [P, KT, E], F16)
        rt_lo = sb("rt_lo", [P, KT, E], F16)
        rstage = sb("rstage", [E, D])
        bstage = sb("bstage", [3 * KT, P])
        pgroup = sb("pgroup", [P, 2, 4, 64])
        ident = sb("ident", [P, P])
        blockmask = sb("blockmask", [P, P])
        ones = sb("ones", [P, P])
        minus_half = sb("minus_half", [P, TT])
        ln_eps = sb("ln_eps", [P, TT])
        scratch = sb("scratch", [P, 2])
        before = sb("before", [P, GROUPS, GROUPS])
        after = sb("after", [P, GROUPS, GROUPS])
        bias_col = sb("bias_col", [P, 3, KT])
        row_bias = sb("row_bias", [P, 4, D])
        ebias = sb("ebias", [P, E])
        x0 = sb("x0", [P, TT, D])
        x1 = sb("x1", [P, TT, D])
        x1b = sb("x1b", [P, TT, D])
        x2 = sb("x2", [P, TT, D])
        xo = sb("xo", [P, TT, D])
        xn = sb("xn", [P, TT, D])
        xt_hi = {stage: sb(f"xt_hi_{stage}", [P, KT, TOK], F16) for stage in ("f1", "at", "f2")}
        xt_lo = {stage: sb(f"xt_lo_{stage}", [P, KT, TOK], F16) for stage in ("f1", "at", "f2")}
        bn = sb("bn", [P, TT, 6])
        mv = sb("mv", [P, TT, 2])
        veps = sb("veps", [P, TT])
        rstd = sb("rstd", [P, TT])
        silu_g = sb("silu_g", [P, 2, TOK])
        prod = sb("prod", [P, 2, TOK])
        h_hi = sb("h_hi", [P, 3, TOK], F16)
        h_lo = sb("h_lo", [P, 3, TOK], F16)
        scores = sb("scores", [P, TT, E])
        biased = sb("biased", [P, TT, E])
        pair_max = sb("pair_max", [P, TT * GROUPS, 2])
        pair_min = sb("pair_min", [P, TT * GROUPS, 2])
        first = sb("first", [P, TT * GROUPS])
        second_a = sb("second_a", [P, TT * GROUPS])
        second_b = sb("second_b", [P, TT * GROUPS])
        second = sb("second", [P, TT * GROUPS])
        gscore = sb("gscore", [P, TT, GROUPS])
        beats_ge = sb("beats_ge", [P, TT, GROUPS, GROUPS])
        beats_gt = sb("beats_gt", [P, TT, GROUPS, GROUPS])
        grank = sb("grank", [P, TT, GROUPS])
        gmask = sb("gmask", [P, TT, GROUPS])
        cand = sb("cand", [P, TT, E + PADS])
        top8 = sb("top8", [P, TT, 8])
        marked = sb("marked", [P, TT, E + PADS])
        chosen = sb("chosen", [P, TT, E])
        wsum = sb("wsum", [P, TT])
        wrec = sb("wrec", [P, TT])
        comb = {stage: sb(f"comb_{stage}", [P, TT, E]) for stage in ("f1", "f2")}
        act32 = sb("act32", [P, 3, KT, TOK])
        staging = act32[:].rearrange("p a k t -> p (a k) t")
        act_hi = sb("act_hi", [P, 3, KT, TOK], F16)
        act_lo = sb("act_lo", [P, 3, KT, TOK], F16)
        gate = sb("gate", [P, TT, D])
        kqx = sb("kqx", [P, 2, TT, D])
        soft = sb("soft", [P, 2, TT * D])
        kq_hi = sb("kq_hi", [P, 2, TT, D], F16)
        kq_lo = sb("kq_lo", [P, 2, TT, D], F16)
        kv = sb("kv", [P, 2, P])
        kvi = sb("kvi", [P, 2, P])
        zden = sb("zden", [P, 2, P])
        zrec = sb("zrec", [P, 2, P])
        mix = sb("mix", [P, 2, P])
        mix_hi = sb("mix_hi", [P, 2, P], F16)
        mix_lo = sb("mix_lo", [P, 2, P], F16)
        og = sb("og", [P, 8, 2, 4, HD])
        ot_hi = sb("ot_hi", [P, 2, HEADS, Q32], F16)
        ot_lo = sb("ot_lo", [P, 2, HEADS, Q32], F16)

        bank = [ctx.enter_context(nc.psum_tensor(f"bank{i}", [P, 512], F32)) for i in range(8)]
        gate_ps, up_ps = bank[0], bank[1]
        down_ps = [bank[2], bank[3]]
        side_ps = bank[4:8]

        w_loaded = [sem(f"w_loaded{i}") for i in range(RING)]
        small_loaded = sem("small_loaded")
        rows_loaded = sem("rows_loaded")
        consts_ready = sem("consts_ready")
        w_turned = sem("w_turned")
        rt_hi_done = sem("rt_hi_done")
        rt_lo_done = sem("rt_lo_done")
        bias_turned = sem("bias_turned")
        small_turned = sem("small_turned")
        w_hi_done = sem("w_hi_done")
        w_lo_done = sem("w_lo_done")
        p_grouped = sem("p_grouped")
        x_loaded = sem("x_loaded")
        stored = sem("stored")
        stats_done = sem("stats_done")
        veps_done = sem("veps_done")
        rstd_done = sem("rstd_done")
        xn_done = sem("xn_done")
        turned = sem("turned")
        xt_hi_done = sem("xt_hi_done")
        xt_lo_done = sem("xt_lo_done")
        logits_done = sem("logits_done")
        scores_done = sem("scores_done")
        route_step = sem("route_step")
        gate_done = sem("gate_done")
        up_done = sem("up_done")
        silu_done = sem("silu_done")
        prod_done = sem("prod_done")
        hi_done = sem("hi_done")
        lo_done = sem("lo_done")
        down_done = sem("down_done")
        comb_done = sem("comb_done")
        proj_done = sem("proj_done")
        gelu_done = sem("gelu_done")
        act_hi_done = sem("act_hi_done")
        act_lo_done = sem("act_lo_done")
        gproj_done = sem("gproj_done")
        gate_biased = sem("gate_biased")
        gate_ready = sem("gate_ready")
        kq2_done = sem("kq2_done")
        kq_biased = sem("kq_biased")
        abs_done = sem("abs_done")
        exp_done = sem("exp_done")
        softplus_done = sem("softplus_done")
        kq_hi_done = sem("kq_hi_done")
        kq_lo_done = sem("kq_lo_done")
        x1b_done = sem("x1b_done")
        kq_summed = sem("kq_summed")
        kv_done = sem("kv_done")
        kv_masked = sem("kv_masked")
        z_done = sem("z_done")
        mix_step = sem("mix_step")
        apply_done = sem("apply_done")
        og_done = sem("og_done")
        regrouped = sem("regrouped")
        ot_hi_done = sem("ot_hi_done")
        ot_lo_done = sem("ot_lo_done")
        project_done = sem("project_done")
        x2_done = sem("x2_done")

        block = ctx.enter_context(nc.Block())

        groups = [g for e in range(0, NE, 2) for g in (("gu", e), ("gu", e + 1), ("dn", e))]
        groups += [("at", a) for a in (K1, Q1, V, K2, Q2, G)] + [("pw", 0)]
        NG = len(groups)
        at_src = {Q1: q_w1, K1: k_w1, V: v_w, G: g_w, Q2: q_w2, K2: k_w2}

        def weight_dmas(kind, i):
            if kind == "gu":
                if i < E:
                    return [((0, 256), gate_w[i]), ((256, 512), up_w[i])]
                row = (i - E) * P
                return [((0, 256), sh_gate_w[row:row + P, :]), ((256, 512), sh_up_w[row:row + P, :])]
            if kind == "dn":
                if i < E:
                    return [((0, 512), down_w[i:i + 2].rearrange("e (h p) i -> p e h i", p=P))]
                return [((256 * j, 256 * j + 256),
                         sh_down_w[:, j * P:(j + 1) * P].rearrange("(h p) i -> p h i", p=P)) for j in range(2)]
            if kind == "at":
                return [((0, 512), at_src[i].rearrange("(h p) i -> p h i", p=P))]
            return [((0, 512), p_w.rearrange("(h p) i -> p h i", p=P))]

        slot_use, loads_of = [0] * RING, []
        for n, (kind, i) in enumerate(groups):
            slot_use[n % RING] += 16 * len(weight_dmas(kind, i))
            loads_of.append(slot_use[n % RING])

        def blocks_of(n):
            kind, i = groups[n]
            st = staging[:, n % RING, :]
            if kind in ("gu", "dn"):
                return [st[:, b * P:(b + 1) * P] for b in range(4)]
            if kind == "at":
                return [st[:, h * 256 + k * P:h * 256 + (k + 1) * P] for k in range(KT) for h in range(2)]
            return [pgroup[:, h, 2 * j2:2 * j2 + 2, :].rearrange("p j n -> p (j n)") for j2 in range(2) for h in range(2)]

        def resident(n):
            kind, i = groups[n]
            if kind == "gu":
                return [t[:, i].rearrange("p m k o -> p (m k o)") for t in (gu_hi, gu_lo)]
            if kind == "dn":
                return [t[:, i:i + 2].rearrange("p e o -> p (e o)") for t in (dn_hi, dn_lo)]
            if kind == "at":
                return [t[:, i].rearrange("p k o -> p (k o)") for t in (at_hi, at_lo)]
            return [t[:].rearrange("p j o -> p (j o)") for t in (pw_hi, pw_lo)]

        def f2_call(s):
            return 2 * s - 2

        def f1_call(s):
            return 2 * s - 1

        xview = x.rearrange("s (t p) d -> s p t d", p=P)
        oview = out.rearrange("s (t p) d -> s p t d", p=P)
        xin = {"f1": x0, "at": x1, "f2": x2}
        xout = {"f1": x1, "f2": xo}

        def pipeline(fori, pieces):
            def do(name, *args):
                if name in pieces:
                    pieces[name](*args)

            def in_slots(slots, e):
                for name, *args in slots.get(e, []):
                    do(name, *args)

            def beside_ffn2(n, f1, p):
                routing = 2 * n + 1
                slots = {0: [("stats", "at", p, n, f1)], 1: [("norm", "at", p), ("add_pb", n, f1)],
                         2: [("turn", "at", p, n), ("turn_hi", "at", p), ("turn_lo", "at", p)],
                         3: [("project_in", n, 0, p, routing)],
                         4: [("project_in", n, 1, p, routing), ("gelu", n, 0)],
                         5: [("project_in", n, 2, p, routing), ("gelu", n, 1), ("split", n, 0)],
                         6: [("split", n, 1)],
                         7: [("second", n, 0), ("gelu", n, 2)],
                         8: [("second", n, 1), ("split", n, 2), ("add_bias", n, 0)],
                         9: [("add_bias", n, 1), ("absolute", n, 0)],
                         10: [("absolute", n, 1), ("project_gate", n, 0), ("softplus_exp", n)],
                         11: [("gate_bias", n, 0)],
                         12: [("project_gate", n, 1), ("softplus_ln", n), ("gate_bias", n, 1)],
                         14: [("finish_kq", n, 0)],
                         15: [("split_kq", n, 0), ("finish_kq", n, 1)],
                         16: [("split_kq", n, 1)]}
                slots[4].append(("stats", "f1", p + 1, n + 1, None))
                slots[6].append(("norm", "f1", p + 1))
                slots[9] += [("turn", "f1", p + 1, n + 1), ("turn_hi", "f1", p + 1)]
                slots[10].append(("turn_lo", "f1", p + 1))
                slots[11] += [("logits", "f1", p + 1, n + 1, routing), ("sigmoid", routing)]
                slots[12] += [("route_scores", routing), ("route_groups", routing)]
                slots[13] = [("route_experts", routing)]
                slots[17] = [("route_weights", "f1", routing)]
                return lambda e: in_slots(slots, e)

            def beside_ffn1(n, p, routing):
                slots = {0: [("kv_sum", n), ("gate_gelu", n)], 1: [("kv_norm", n)], 2: [("mix", n)],
                         3: [("apply", n, routing)], 4: [("gate_out", n)],
                         5: [("regroup", n), ("split_out", n, 0)], 6: [("split_out", n, 1)],
                         7: [("project_out", n), ("residual", n)],
                         8: [("stats", "f2", p, n, None)], 9: [("norm", "f2", p)],
                         10: [("turn", "f2", p, n), ("turn_hi", "f2", p), ("turn_lo", "f2", p)],
                         11: [("logits", "f2", p, n, routing)], 12: [("sigmoid", routing)],
                         13: [("route_scores", routing)], 14: [("route_groups", routing)],
                         15: [("route_experts", routing)], 17: [("route_weights", "f2", routing)]}
                return lambda e: in_slots(slots, e)

            def attention_slots(n, p, routed):
                return {0: [("norm", "at", p), ("add_pb", n, 2 * n - 1 if n else 0)],
                        1: [("turn", "at", p, n), ("turn_hi", "at", p), ("turn_lo", "at", p)],
                        2: [("project_in", n, 0, p, routed), ("gelu", n, 0),
                            ("project_in", n, 1, p, routed), ("gelu", n, 1)],
                        3: [("project_in", n, 2, p, routed), ("gelu", n, 2), ("split", n, 0)],
                        4: [("second", n, 0), ("split", n, 1)],
                        5: [("split", n, 2), ("add_bias", n, 0), ("second", n, 1), ("add_bias", n, 1), ("absolute", n, 0)],
                        6: [("absolute", n, 1), ("project_gate", n, 0), ("softplus_exp", n)],
                        7: [("gate_bias", n, 0)],
                        8: [("project_gate", n, 1), ("softplus_ln", n), ("gate_bias", n, 1), ("finish_kq", n, 0)],
                        9: [("finish_kq", n, 1), ("split_kq", n, 0)],
                        10: [("split_kq", n, 1)],
                        11: [("kv_sum", n), ("gate_gelu", n)],
                        12: [("kv_norm", n), ("mix", n)],
                        13: [("apply", n, routed)],
                        14: [("gate_out", n)],
                        15: [("regroup", n), ("split_out", n, 0), ("split_out", n, 1)],
                        16: [("project_out", n), ("residual", n), ("stats", "f2", p + 1, n, None), ("norm", "f2", p + 1)]}

            def prologue_end(n, p, routing):
                do("turn", "f2", p, n)
                do("turn_hi", "f2", p)
                do("turn_lo", "f2", p)
                do("logits", "f2", p, n, routing)
                do("sigmoid", routing)

            do("stats", "f1", 0, 0, None)
            do("weights", 0, 1)
            do("norm", "f1", 0)
            do("weights", 1, FIRST_GROUPS - 1)
            do("turn", "f1", 0, 0)
            do("turn_hi", "f1", 0)
            do("turn_lo", "f1", 0)
            do("small_weights")
            do("weights", FIRST_GROUPS - 1, FIRST_GROUPS)
            do("logits", "f1", 0, 0, 0)
            do("sigmoid", 0)
            first = {e: [("weights", FIRST_GROUPS + 2 * e, FIRST_GROUPS + 2 * e + 2)] for e in range(NE)}
            first[0] += [("route_scores", 0), ("route_groups", 0)]
            first[1] += [("route_experts", 0), ("route_weights", "f1", 0)]
            first[13] += [("stats", "f1", 1, 1, None)]
            first[15] += [("norm", "f1", 1)]
            first[17] += [("turn", "f1", 1, 1), ("turn_hi", "f1", 1)]
            do("ffn", "f1", 0, 0, 0, None, lambda e: in_slots(first, e))
            do("turn_lo", "f1", 1)
            do("finish", "f1", 0)
            do("logits", "f1", 1, 1, 1)
            do("sigmoid", 1)
            do("stats", "at", 2, 0, 0)
            table = attention_slots(n=0, p=2, routed=2)
            table[0] += [("route_scores", 1)]
            table[1] += [("route_groups", 1), ("route_experts", 1), ("route_weights", "f1", 1)]
            do("ffn", "f1", 1, 1, 1, None, lambda e: in_slots(table, e))
            prologue_end(n=0, p=3, routing=2)
            for name, *args in (("route_scores", 2), ("route_groups", 2), ("route_experts", 2), ("route_weights", "f2", 2)):
                do(name, *args)
            with fori(2, SEQS) as s:
                do("ffn", "f2", 2 * s - 2, s - 2, 3 * s - 3, "f1",
                   beside_ffn2(n=s - 1, f1=2 * s - 3, p=3 * s - 2))
                do("ffn", "f1", 2 * s - 1, s, 3 * s - 1, "f2", beside_ffn1(n=s - 1, p=3 * s, routing=2 * s))
            last = SEQS - 1
            table = attention_slots(n=last, p=3 * last + 1, routed=2 * last + 1)
            later = {e + 1: names for e, names in table.items()}
            later[0] = [("stats", "at", 3 * last + 1, last, 2 * last - 1)]
            do("ffn", "f2", 2 * last, last - 1, 3 * last, "f1", lambda e: in_slots(later, e))
            do("finish", "f2", 2 * last)
            prologue_end(n=last, p=3 * last + 2, routing=2 * last + 1)
            table = {0: [("route_scores", 2 * last + 1), ("route_groups", 2 * last + 1)],
                     1: [("route_experts", 2 * last + 1), ("route_weights", "f2", 2 * last + 1)]}
            do("ffn", "f2", 2 * last + 1, last, 3 * last + 2, None, lambda e: in_slots(table, e))
            do("finish", "f2", 2 * last + 1)

        def quarters(b, ot):
            for half in range(2):
                for j1 in range(2):
                    head = 8 * half + 4 * b
                    yield (side_ps[b][64 * half:64 * half + 64, :]
                           .rearrange("p (h j2 j1 q) -> p h j2 j1 q", h=4, j2=2, j1=2)[:, :, :, j1, :],
                           ot[64 * j1:64 * j1 + 64, :, head:head + 4, :].rearrange("p j2 h q -> p h j2 q"))

        def weights_ps(n):
            return bank[n] if n < FIRST_GROUPS else side_ps[n % 4]

        def turn_ps(stage, k):
            return side_ps[2 + k] if stage == "f1" else side_ps[k]

        def known_zero(v):
            return isinstance(v, int) and v == 0

        @block.sync
        def _(sp):
            sp.dma_start(x0[:], xview[0]).then_inc(x_loaded, 16)
            for n, (kind, i) in enumerate(groups):
                if n >= RING:
                    sp.wait_ge(w_turned, n - RING + 1)
                for (a, b), src in weight_dmas(kind, i):
                    dst = staging[:, n % RING, a:b]
                    if len(src.shape) == 3:
                        dst = dst.rearrange("p (h i) -> p h i", h=src.shape[1])
                    if len(src.shape) == 4:
                        dst = dst.rearrange("p (e h i) -> p e h i", e=2, h=2)
                    sp.dma_start(dst, src).then_inc(w_loaded[n % RING], 16)
                if n == RING - 1:
                    for i, b in enumerate((g_b, k_b2, q_b2, p_b)):
                        sp.dma_start(row_bias[:, i, :], b.partition_broadcast(P)).then_inc(rows_loaded, 16)

            def load_x(n, f):
                sp.wait_ge(comb_done, COMB_EV * f + TT)
                sp.dma_start(x0[:], xview[n]).then_inc(x_loaded, 16)

            def store_x(n, f):
                sp.wait_ge(comb_done, COMB_EV * (f + 1))
                sp.dma_start(oview[n], xo[:]).then_inc(stored, 16)

            load_x(1, 0)
            load_x(2, 1)
            with sp.Fori(2, SEQS - 1) as s:
                store_x(s - 2, f2_call(s))
                load_x(s + 1, f1_call(s))
            store_x(SEQS - 3, f2_call(SEQS - 1))
            store_x(SEQS - 2, f2_call(SEQS))
            store_x(SEQS - 1, 2 * SEQS - 1)
            sp.wait_ge(stored, 16 * SEQS)

        @block.tensor
        def _(pe):
            def three(out_ap, pairs):
                n = len(pairs)
                for i, (a_hi, a_lo, b_hi, b_lo) in enumerate(pairs):
                    pe.matmul(out_ap, a_hi, b_hi, start=(i == 0), stop=False)
                    pe.matmul(out_ap, a_hi, b_lo, start=False, stop=False)
                    last = pe.matmul(out_ap, a_lo, b_hi, start=False, stop=(i == n - 1))
                return last

            def weights(first, stop):
                for n in range(first, min(stop, NG)):
                    if groups[n][0] == "pw":
                        pe.wait_ge(p_grouped, 2)
                    else:
                        pe.wait_ge(w_loaded[n % RING], loads_of[n])
                    if n == FIRST_GROUPS:
                        pe.wait_ge(scores_done, 1)
                    if n >= FIRST_GROUPS + 4:
                        pe.wait_ge(w_lo_done, n - 3)
                    for b, src in enumerate(blocks_of(n)):
                        last = pe.transpose(weights_ps(n)[:, b * P:(b + 1) * P], src, ident[:])
                    last.then_inc(w_turned, 1)

            def turn(stage, p, n):
                pe.wait_ge(xn_done, p + 1)
                if not known_zero(p):
                    pe.wait_ge(xt_hi_done, 2 * p)
                    pe.wait_ge(xt_lo_done, 2 * p)
                if stage == "f1" and not isinstance(n, int):
                    pe.wait_ge(kq_biased, 4 * n - 2)
                for k in range(KT):
                    for t in range(TT):
                        last = pe.transpose(turn_ps(stage, k)[:, t * P:(t + 1) * P], xn[:, t, k * P:(k + 1) * P], ident[:])
                    last.then_inc(turned, 1)

            def logits(stage, p, n, routing):
                pe.wait_ge(xt_hi_done, 2 * p + 2)
                pe.wait_ge(xt_lo_done, 2 * p + 2)
                for t in range(TT):
                    c = slice(t * P, (t + 1) * P)
                    last = three(side_ps[2][:, t * E:(t + 1) * E],
                                 [(xt_hi[stage][:, k, c], xt_lo[stage][:, k, c], rt_hi[:, k, :], rt_lo[:, k, :])
                                  for k in range(KT)])
                last.then_inc(logits_done, 1)

            def down(f, e):
                last_e = e if e < E else E + SHARED - 1
                pe.wait_ge(hi_done, NE * f + last_e + 1)
                pe.wait_ge(lo_done, NE * f + last_e + 1)
                for b in range(2):
                    if e > 0 or not known_zero(f):
                        pe.wait_ge(comb_done, COMB_EV * f + TT * (e - 1) + 2 * b + 2)
                    for t in (2 * b, 2 * b + 1):
                        c = slice(t * P, (t + 1) * P)
                        dst = down_ps[b][:, (t % 2) * D:(t % 2 + 1) * D]
                        h_h, h_l = h_hi[:, e % 3, c], h_lo[:, e % 3, c]
                        if e < E:
                            pe.matmul(dst, h_h, dn_hi[:, e, :], start=True, stop=False)
                            pe.matmul(dst, h_h, dn_lo[:, e, :], start=False, stop=False)
                            last = pe.matmul(dst, h_l, dn_hi[:, e, :], start=False, stop=True)
                        else:
                            for i, j in enumerate((E, E + 1)):
                                a_h, a_l = h_hi[:, j % 3, c], h_lo[:, j % 3, c]
                                pe.matmul(dst, a_h, dn_hi[:, j, :], start=(i == 0), stop=False)
                                pe.matmul(dst, a_h, dn_lo[:, j, :], start=False, stop=False)
                                last = pe.matmul(dst, a_l, dn_hi[:, j, :], start=False, stop=(i == 1))
                    last.then_inc(down_done, 1)

            def ffn(stage, f, n, p, previous, side):
                pe.wait_ge(xt_hi_done, 2 * p + 2)
                pe.wait_ge(xt_lo_done, 2 * p + 2)
                for e in range(NE):
                    g = NE * f + e
                    if known_zero(f):
                        pe.wait_ge(w_lo_done, max(groups.index(("gu", e)) + 1, 2))
                        if e >= 2:
                            pe.wait_ge(w_lo_done, groups.index(("dn", (e - 2) // 2 * 2)) + 1)
                    if e > 0 or not known_zero(f):
                        pe.wait_ge(silu_done, g)
                    three(gate_ps[:], [(gu_hi[:, e, 0, k], gu_lo[:, e, 0, k], xt_hi[stage][:, k], xt_lo[stage][:, k])
                                       for k in range(KT)]).then_inc(gate_done, 1)
                    if e > 0 or not known_zero(f):
                        pe.wait_ge(prod_done, g)
                    three(up_ps[:], [(gu_hi[:, e, 1, k], gu_lo[:, e, 1, k], xt_hi[stage][:, k], xt_lo[stage][:, k])
                                     for k in range(KT)]).then_inc(up_done, 1)
                    if e == 0 and previous is not None:
                        down(f - 1, E)
                    if e >= 2:
                        down(f, e - 2)
                    side(e)

            def finish(stage, f):
                down(f, E)

            def project_in(n, i, p, routed):
                if i == 0:
                    pe.wait_ge(xt_hi_done, 2 * p + 2)
                    pe.wait_ge(xt_lo_done, 2 * p + 2)
                    if known_zero(n):
                        pe.wait_ge(w_lo_done, NG)
                if i == 1:
                    pe.wait_ge(scores_done, routed)
                if i == 2:
                    pe.wait_ge(gelu_done, 6 * n + 2)
                for h in range(2):
                    o = slice(h * P, (h + 1) * P)
                    a = (K1, Q1, V)[i]
                    three(side_ps[(0, 2, 0)[i] + h][:],
                          [(at_hi[:, a, k, o], at_lo[:, a, k, o], xt_hi["at"][:, k], xt_lo["at"][:, k])
                           for k in range(KT)]).then_inc(proj_done, 1)

            def second(n, i):
                pe.wait_ge(act_lo_done, 6 * n + 2 * i + 2)
                pe.wait_ge(gelu_done, 6 * n + 2 * i + 4)
                for t in range(TT):
                    c = slice(t * P, (t + 1) * P)
                    last = three(side_ps[(2, 0)[i] + t // 2][:, (t % 2) * D:(t % 2 + 1) * D],
                                 [(act_hi[:, i, k, c], act_lo[:, i, k, c],
                                   at_hi[:, (K2, Q2)[i], k], at_lo[:, (K2, Q2)[i], k]) for k in range(KT)])
                    if t % 2:
                        last.then_inc(kq2_done, 1)

            def project_gate(n, b):
                pe.wait_ge(kq_biased, 4 * n + 4)
                for t in (2 * b, 2 * b + 1):
                    c = slice(t * P, (t + 1) * P)
                    last = three(side_ps[b][:, (t % 2) * D:(t % 2 + 1) * D],
                                 [(xt_hi["at"][:, k, c], xt_lo["at"][:, k, c], at_hi[:, G, k], at_lo[:, G, k])
                                  for k in range(KT)])
                last.then_inc(gproj_done, 1)

            def kv_sum(n):
                pe.wait_ge(kq_lo_done, 2 * n + 2)
                pe.wait_ge(gate_biased, 2 * n + 2)
                for h in range(2):
                    c = slice(h * P, (h + 1) * P)
                    last = three(side_ps[0][:, h * P:(h + 1) * P],
                                 [(kq_hi[:, 0, t, c], kq_lo[:, 0, t, c], kq_hi[:, 1, t, c], kq_lo[:, 1, t, c])
                                  for t in range(TT)])
                last.then_inc(kv_done, 1)

            def kv_norm(n):
                pe.wait_ge(kv_masked, n + 1)
                pe.matmul(side_ps[1][:, 0:D], ones[:], kv[:].rearrange("p h m -> p (h m)"),
                          start=True, stop=True).then_inc(z_done, 1)

            def apply(n, routing):
                pe.wait_ge(mix_step, MIX_STEPS * (n + 1))
                pe.wait_ge(act_lo_done, 6 * n + 6)
                pe.wait_ge(scores_done, routing)
                for t in range(TT):
                    c = slice(t * P, (t + 1) * P)
                    for h in range(2):
                        last = three(side_ps[2 + t // 2][:, (t % 2) * D + h * P:(t % 2) * D + (h + 1) * P],
                                     [(act_hi[:, 2, h, c], act_lo[:, 2, h, c], mix_hi[:, h], mix_lo[:, h])])
                    if t % 2:
                        last.then_inc(apply_done, 1)

            def regroup(n):
                pe.wait_ge(og_done, TT * n + TT)
                for hh in range(8):
                    last = pe.transpose(side_ps[hh // 4][:, (hh % 4) * P:(hh % 4 + 1) * P],
                                        og[:, hh].rearrange("p h j n -> p (h j n)"), ident[:])
                    if hh % 4 == 3:
                        last.then_inc(regrouped, 1)

            def project_out(n):
                pe.wait_ge(ot_hi_done, 2 * n + 2)
                pe.wait_ge(ot_lo_done, 2 * n + 2)
                for t in range(TT):
                    last = three(side_ps[2 + t // 2][:, (t % 2) * D:(t % 2 + 1) * D],
                                 [(ot_hi[:, j, 4 * t:4 * t + 4, :].rearrange("p h q -> p (h q)"),
                                   ot_lo[:, j, 4 * t:4 * t + 4, :].rearrange("p h q -> p (h q)"),
                                   pw_hi[:, j], pw_lo[:, j]) for j in range(2)])
                    if t % 2:
                        last.then_inc(project_done, 1)

            def small_weights():
                pe.wait_ge(small_loaded, SMALL)
                for k in range(KT):
                    pe.transpose(side_ps[0][:, k * E:(k + 1) * E], rstage[:, k * P:(k + 1) * P], ident[0:E, 0:E])
                pe.transpose(side_ps[0][:, KT * E:KT * E + 3 * KT], bstage[:],
                             ident[0:3 * KT, 0:3 * KT]).then_inc(small_turned, 1)
                pe.wait_ge(rt_lo_done, 1)
                pe.wait_ge(bias_turned, 1)

            pe.wait_ge(consts_ready, CONSTS)
            pipeline(pe.Fori, dict(small_weights=small_weights, weights=weights, turn=turn, logits=logits,
                                   ffn=ffn, finish=finish,
                                   project_in=project_in, second=second, project_gate=project_gate, kv_sum=kv_sum,
                                   kv_norm=kv_norm, apply=apply, regroup=regroup, project_out=project_out))

        @block.scalar
        def _(act):
            for i, (b, dst) in enumerate(((q_b1, 1), (k_b1, 0), (v_b, 2))):
                act.dma_start(bstage[dst * KT:(dst + 1) * KT, :], b.rearrange("(k p) -> k p", p=P)).then_inc(small_loaded, 16)
            act.dma_start(ebias[:], e_bias.partition_broadcast(P)).then_inc(small_loaded, 16)
            act.dma_start(rstage[:], router_w).then_inc(small_loaded, 16)

            def small_weights():
                act.wait_ge(small_turned, 1)
                act.activation(rt_hi[:].rearrange("p k e -> p (k e)"), side_ps[0][:, 0:KT * E], ACT.Copy,
                               scale=W_SCALE).then_inc(rt_hi_done, 1)
                act.activation(bias_col[:].rearrange("p b k -> p (b k)"), side_ps[0][:, KT * E:KT * E + 3 * KT],
                               ACT.Copy).then_inc(bias_turned, 1)
                act.wait_ge(bias_turned, 1)

            def weights(first, stop):
                for n in range(first, min(stop, NG)):
                    act.wait_ge(w_turned, n + 1)
                    act.activation(resident(n)[0], weights_ps(n)[:], ACT.Copy, scale=W_SCALE).then_inc(w_hi_done, 1)

            def turn_hi(stage, p):
                for k in range(KT):
                    act.wait_ge(turned, 2 * p + k + 1)
                    src = turn_ps(stage, k)[:]
                    dst = xt_hi[stage][:, k]
                    if stage == "at":
                        src = src.rearrange("p (q j) -> p j q", j=J16)
                        dst = dst.rearrange("p (j q) -> p j q", j=J16)
                    act.activation(dst, src, ACT.Copy).then_inc(xt_hi_done, 1)

            def sigmoid(routing):
                act.wait_ge(logits_done, routing + 1)
                if not known_zero(routing):
                    act.wait_ge(route_step, ROUTE_STEPS * routing)
                act.activation(scores[:].rearrange("p t e -> p (t e)"), side_ps[2][:, 0:TT * E], ACT.Tanh,
                               scale=0.5 * INV_W).then_inc(scores_done, 1)

            def ffn(stage, f, n, p, previous, side):
                for e in range(NE):
                    g = NE * f + e
                    act.wait_ge(gate_done, g + 1)
                    if e >= 2 or not known_zero(f):
                        act.wait_ge(prod_done, g - 1)
                    act.activation(silu_g[:, e % 2], gate_ps[:], ACT.Silu, scale=INV_W).then_inc(silu_done, 1)
                    act.wait_ge(prod_done, g + 1)
                    if e >= 3:
                        act.wait_ge(down_done, DOWN_EV * f + 2 * (e - 2))
                    elif not known_zero(f):
                        act.wait_ge(down_done, DOWN_EV * f - (2 if e == 0 else 0))
                    act.activation(h_hi[:, e % 3], prod[:, e % 2], ACT.Copy).then_inc(hi_done, 1)
                    side(e)

            def gelu(n, i):
                for h in range(2):
                    act.wait_ge(proj_done, 6 * n + 2 * i + h + 1)
                    if not known_zero(n):
                        act.wait_ge(act_lo_done, 6 * n)
                    act.activation(act32[:, i, h], side_ps[(0, 2, 0)[i] + h][:], ACT.Gelu, scale=INV_W,
                                   bias=bias_col[:, i, h:h + 1]).then_inc(gelu_done, 1)

            def absolute(n, i):
                act.wait_ge(kq_biased, 4 * n + 2 * i + 2)
                if not known_zero(n):
                    act.wait_ge(kq_summed, 2 * n)
                act.activation(soft[:, i], kqx[:, i].rearrange("p t d -> p (t d)"), ACT.Abs).then_inc(abs_done, 1)

            def softplus_exp(n):
                for i in range(2):
                    act.wait_ge(abs_done, 2 * n + i + 1)
                    act.activation(soft[:, i], soft[:, i], ACT.Exp, scale=-1.0).then_inc(exp_done, 1)

            def softplus_ln(n):
                for i in range(2):
                    act.wait_ge(exp_done, 2 * n + i + 1)
                    act.activation(soft[:, i], soft[:, i], ACT.Ln, bias=1.0).then_inc(softplus_done, 1)

            def split_kq(n, i):
                act.wait_ge(kq_summed, 2 * n + i + 1)
                if not known_zero(n):
                    act.wait_ge(kv_done, n)
                    act.wait_ge(kq_lo_done, 2 * n)
                act.activation(kq_hi[:, i], kqx[:, i], ACT.Copy).then_inc(kq_hi_done, 1)

            def gate_gelu(n):
                for b in range(2):
                    act.wait_ge(gate_biased, 2 * n + b + 1)
                    act.activation(gate[:, 2 * b:2 * b + 2], gate[:, 2 * b:2 * b + 2], ACT.Gelu).then_inc(gate_ready, 1)

            def split_out(n, b):
                act.wait_ge(regrouped, 2 * n + b + 1)
                for src, hi in quarters(b, ot_hi):
                    ins = act.activation(hi, src, ACT.Copy)
                ins.then_inc(ot_hi_done, 1)

            pipeline(act.Fori, dict(small_weights=small_weights, weights=weights, turn_hi=turn_hi,
                                    sigmoid=sigmoid, ffn=ffn, gelu=gelu,
                                    absolute=absolute, split_kq=split_kq, softplus_exp=softplus_exp, softplus_ln=softplus_ln,
                                    gate_gelu=gate_gelu, split_out=split_out))
            act.wait_ge(stored, 16 * SEQS)

        @block.gpsimd
        def _(pool):
            pool.memset(ident[:], 0.0).then_inc(consts_ready, 1)
            pool.wait_ge(consts_ready, 1)
            pool.affine_select(out=ident[:], in_=ident[:], compare_op=ALU.not_equal, fill=1.0, base=0,
                               pattern=[[-1, P]], channel_multiplier=1).then_inc(consts_ready, 1)
            pool.memset(ones[:], 1.0).then_inc(consts_ready, 1)
            pool.wait_ge(consts_ready, 3)
            bm = blockmask[:].rearrange("p (b c) -> p b c", c=HD)
            on = ones[:].rearrange("p (b c) -> p b c", c=HD)
            pool.affine_select(out=bm, in_=on, compare_op=ALU.is_ge, fill=0.0, base=0,
                               pattern=[[-HD, P // HD], [0, HD]], channel_multiplier=1).then_inc(consts_ready, 1)
            pool.wait_ge(consts_ready, 4)
            pool.affine_select(out=bm, in_=bm, compare_op=ALU.is_ge, fill=0.0, base=HD - 1,
                               pattern=[[HD, P // HD], [0, HD]], channel_multiplier=-1).then_inc(consts_ready, 1)
            pool.memset(minus_half[:], -0.5).then_inc(consts_ready, 1)
            pool.memset(ln_eps[:], LN_EPS).then_inc(consts_ready, 1)
            one_g = ones[:, 0:GROUPS * GROUPS].rearrange("p (g j) -> p g j", j=GROUPS)
            pool.affine_select(out=before[:], in_=one_g, compare_op=ALU.is_ge, fill=0.0, base=-1,
                               pattern=[[1, GROUPS], [-1, GROUPS]], channel_multiplier=0).then_inc(consts_ready, 1)
            pool.affine_select(out=after[:], in_=one_g, compare_op=ALU.is_ge, fill=0.0, base=-1,
                               pattern=[[-1, GROUPS], [1, GROUPS]], channel_multiplier=0).then_inc(consts_ready, 1)
            pool.memset(cand[:], SENTINEL).then_inc(consts_ready, 1)
            pool.wait_ge(consts_ready, CONSTS)

            def stats(stage, p, n, f):
                pool.wait_ge(stats_done, 2 * p + 2)
                pool.tensor_tensor(veps[:], mv[:, :, 1], ln_eps[:], ALU.add).then_inc(veps_done, 1)
                pool.wait_ge(veps_done, p + 1)
                if not known_zero(p):
                    pool.wait_ge(xn_done, p)
                pool.tensor_tensor(rstd[:], veps[:], minus_half[:], ALU.pow).then_inc(rstd_done, 1)

            def ffn(stage, f, n, p, previous, side):
                for e in range(NE):
                    g = NE * f + e
                    pool.wait_ge(hi_done, g + 1)
                    pool.tensor_tensor(h_lo[:, e % 3], prod[:, e % 2], h_hi[:, e % 3], ALU.subtract).then_inc(lo_done, 1)
                    side(e)

            def add_pb(n, f1):
                pool.wait_ge(comb_done, COMB_EV * (f1 + 1))
                if known_zero(n):
                    pool.wait_ge(rows_loaded, ROWS)
                else:
                    pool.wait_ge(x2_done, 2 * n)
                pool.tensor_tensor(x1b[:], x1[:], row_bias[:, 3:4, :].broadcast_to([P, TT, D]),
                                   ALU.add).then_inc(x1b_done, 1)

            def split(n, i):
                for h in range(2):
                    pool.wait_ge(act_hi_done, 6 * n + 2 * i + h + 1)
                    pool.tensor_tensor(act_lo[:, i, h], act32[:, i, h], act_hi[:, i, h],
                                       ALU.subtract).then_inc(act_lo_done, 1)

            def split_kq(n, i):
                pool.wait_ge(kq_hi_done, 2 * n + i + 1)
                pool.tensor_tensor(kq_lo[:, i], kqx[:, i], kq_hi[:, i], ALU.subtract).then_inc(kq_lo_done, 1)

            pipeline(pool.Fori, dict(stats=stats, ffn=ffn, add_pb=add_pb, split=split, split_kq=split_kq))

        @block.vector
        def _(dve):
            def flat(ap):
                return ap.rearrange("p a b -> p (a b)")

            n_pw = groups.index(("pw", 0))
            dve.wait_ge(consts_ready, CONSTS)

            def small_weights():
                dve.wait_ge(rt_hi_done, 1)
                dve.wait_ge(bias_turned, 1)
                dve.scalar_tensor_tensor(out=flat(rt_lo[:]), in0=side_ps[0][:, 0:KT * E], scalar=W_SCALE, in1=flat(rt_hi[:]),
                                         op0=ALU.mult, op1=ALU.subtract).then_inc(rt_lo_done, 1)
                dve.wait_ge(small_loaded, SMALL)

            def weights(first, stop):
                for n in range(first, min(stop, NG)):
                    dve.wait_ge(w_hi_done, n + 1)
                    hi, lo = resident(n)
                    dve.scalar_tensor_tensor(out=lo, in0=weights_ps(n)[:], scalar=W_SCALE, in1=hi,
                                             op0=ALU.mult, op1=ALU.subtract).then_inc(w_lo_done, 1)
                    if n == n_pw - 2:
                        dve.wait_ge(w_loaded[n_pw % RING], loads_of[n_pw])
                        for h in range(2):
                            src = staging[:, n_pw % RING, h * 256:(h + 1) * 256].rearrange("p (J j n) -> p j J n", J=4, j=4)
                            dve.tensor_copy(pgroup[:, h].rearrange("p j (J n) -> p j J n", J=4), src).then_inc(p_grouped, 1)

            def stats(stage, p, n, f):
                src = xin[stage]
                if stage == "f1":
                    dve.wait_ge(x_loaded, 16 * (n + 1))
                elif stage == "at":
                    dve.wait_ge(comb_done, COMB_EV * (f + 1))
                else:
                    dve.wait_ge(x2_done, 2 * (n + 1))
                for t in range(TT):
                    ins = dve.bn_stats(bn[:, t, :], src[:, t, :])
                ins.then_inc(stats_done, 1)
                dve.wait_ge(stats_done, 2 * p + 1)
                dve.memset(scratch[:, 0:1], 0.0)
                for t in range(TT):
                    ins = dve.bn_aggr(mv[:, t, :], bn[:, t, :])
                ins.then_inc(stats_done, 1)

            def norm(stage, p):
                dve.wait_ge(rstd_done, p + 1)
                if not known_zero(p):
                    dve.wait_ge(turned, 2 * p)
                for t in range(TT):
                    ins = dve.tensor_scalar(xn[:, t, :], xin[stage][:, t, :], mv[:, t, 0:1], rstd[:, t:t + 1],
                                            ALU.subtract, ALU.mult)
                ins.then_inc(xn_done, 1)

            def turn_lo(stage, p):
                for k in range(KT):
                    dve.wait_ge(xt_hi_done, 2 * p + k + 1)
                    src, hi, lo = turn_ps(stage, k)[:], xt_hi[stage][:, k], xt_lo[stage][:, k]
                    if stage == "at":
                        src = src.rearrange("p (q j) -> p j q", j=J16)
                        hi, lo = (a.rearrange("p (j q) -> p j q", j=J16) for a in (hi, lo))
                    dve.tensor_tensor(lo, src, hi, ALU.subtract).then_inc(xt_lo_done, 1)

            def route_link(routing, k, ins):
                ins.then_inc(route_step, 1)
                dve.wait_ge(route_step, ROUTE_STEPS * routing + k)

            def route_scores(routing):
                dve.wait_ge(scores_done, routing + 1)
                route_link(routing, 1, dve.tensor_scalar(flat(scores[:]), flat(scores[:]), 0.5, 0.5, ALU.mult, ALU.add))
                route_link(routing, 2, dve.tensor_tensor(biased[:], scores[:], ebias[:].unsqueeze(1).broadcast_to([P, TT, E]), ALU.add))
                by_group = flat(biased[:]).rearrange("p (g e) -> p g e", e=EG)
                dve.tensor_tensor(pair_max[:], by_group[:, :, 0:2], by_group[:, :, 2:4], ALU.max)
                route_link(routing, 3, dve.tensor_tensor(pair_min[:], by_group[:, :, 0:2], by_group[:, :, 2:4], ALU.min))

            def route_groups(routing):
                dve.tensor_tensor(first[:], pair_max[:, :, 0], pair_max[:, :, 1], ALU.max)
                dve.tensor_tensor(second_a[:], pair_max[:, :, 0], pair_max[:, :, 1], ALU.min)
                route_link(routing, 4, dve.tensor_tensor(second_b[:], pair_min[:, :, 0], pair_min[:, :, 1], ALU.max))
                route_link(routing, 5, dve.tensor_tensor(second[:], second_a[:], second_b[:], ALU.max))
                route_link(routing, 6, dve.tensor_tensor(flat(gscore[:]), first[:], second[:], ALU.add))
                other = gscore[:].unsqueeze(2).broadcast_to([P, TT, GROUPS, GROUPS])
                own = gscore[:].unsqueeze(3).broadcast_to([P, TT, GROUPS, GROUPS])
                dve.tensor_tensor(beats_ge[:], other, own, ALU.is_ge)
                route_link(routing, 7, dve.tensor_tensor(beats_gt[:], other, own, ALU.is_gt))
                dve.tensor_tensor(beats_ge[:], beats_ge[:], before[:].unsqueeze(1).broadcast_to([P, TT, GROUPS, GROUPS]), ALU.mult)
                route_link(routing, 8, dve.tensor_tensor(beats_gt[:], beats_gt[:],
                                                   after[:].unsqueeze(1).broadcast_to([P, TT, GROUPS, GROUPS]), ALU.mult))
                route_link(routing, 9, dve.tensor_tensor(beats_ge[:], beats_ge[:], beats_gt[:], ALU.add))

            def route_experts(routing):
                route_link(routing, 10, dve.tensor_reduce(grank[:], beats_ge[:], AX_X, ALU.add))
                route_link(routing, 11, dve.tensor_scalar(flat(gmask[:]), flat(grank[:]), float(TOPG), None, ALU.is_lt))
                route_link(routing, 12, dve.tensor_tensor(
                    cand[:, :, 0:E].rearrange("p t (g e) -> p t g e", e=EG), biased[:].rearrange("p t (g e) -> p t g e", e=EG),
                    gmask[:].unsqueeze(3).broadcast_to([P, TT, GROUPS, EG]), ALU.mult))
                dve.memset(scratch[:, 1:2], 0.0)
                for t in range(TT):
                    ins = dve.max(top8[:, t, :], cand[:, t, :])
                route_link(routing, 13, ins)
                route_link(routing, 14, dve.memset(top8[:, :, TOPK:8], SENTINEL))
                dve.memset(scratch[:, 1:2], 0.0)
                for t in range(TT):
                    ins = dve.match_replace(out=marked[:, t, :], in_to_replace=top8[:, t, :], in_values=cand[:, t, :],
                                            imm_value=MARK)
                route_link(routing, 15, ins)

            def route_weights(stage, routing):
                route_link(routing, 16, dve.tensor_scalar(chosen[:], marked[:, :, 0:E], MARK, None, ALU.is_equal))
                route_link(routing, 17, dve.tensor_tensor(chosen[:], chosen[:], scores[:], ALU.mult))
                route_link(routing, 18, dve.tensor_reduce(wsum[:], chosen[:], AX_X, ALU.add))
                route_link(routing, 19, dve.tensor_scalar(wsum[:], wsum[:], 1e-20, None, ALU.add))
                route_link(routing, 20, dve.reciprocal(wrec[:], wsum[:]))
                route_link(routing, 21, dve.tensor_tensor(chosen[:], chosen[:], wrec[:].unsqueeze(2).broadcast_to([P, TT, E]), ALU.mult))
                route_link(routing, 22, dve.tensor_scalar(comb[stage][:], chosen[:], ROUTE_SCALE * HALF * INV_W, None, ALU.mult))

            def combine(stage, f, e):
                src, dst = (xin[stage] if e == 0 else xout[stage]), xout[stage]
                for t in range(TT):
                    if t % 2 == 0:
                        dve.wait_ge(down_done, DOWN_EV * f + 2 * e + t // 2 + 1)
                    if e > 0:
                        dve.wait_ge(comb_done, COMB_EV * f + TT * (e - 1) + t + 1)
                    weight = comb[stage][:, t, e:e + 1] if e < E else HALF * INV_W
                    dve.scalar_tensor_tensor(out=dst[:, t, :], in0=down_ps[t // 2][:, (t % 2) * D:(t % 2 + 1) * D],
                                             scalar=weight, in1=src[:, t, :], op0=ALU.mult,
                                             op1=ALU.add).then_inc(comb_done, 1)

            def ffn(stage, f, n, p, previous, side):
                for e in range(NE):
                    g = NE * f + e
                    dve.wait_ge(up_done, g + 1)
                    dve.wait_ge(silu_done, g + 1)
                    if e >= 2 or not known_zero(f):
                        dve.wait_ge(lo_done, g - 1)
                    dve.scalar_tensor_tensor(out=prod[:, e % 2], in0=up_ps[:], scalar=INV_W, in1=silu_g[:, e % 2],
                                             op0=ALU.mult, op1=ALU.mult).then_inc(prod_done, 1)
                    if e == 0 and previous is not None:
                        combine(previous, f - 1, E)
                    if e == 2:
                        if stage == "f1" and not known_zero(n):
                            dve.wait_ge(x1b_done, n)
                        if stage == "f2" and not known_zero(n):
                            dve.wait_ge(stored, 16 * n)
                    if e >= 2:
                        combine(stage, f, e - 2)
                    side(e)

            def finish(stage, f):
                combine(stage, f, E)

            def split(n, i):
                for h in range(2):
                    dve.wait_ge(gelu_done, 6 * n + 2 * i + h + 1)
                    if not known_zero(n):
                        dve.wait_ge(apply_done, 2 * n)
                        dve.wait_ge(act_lo_done, 6 * n)
                    dve.tensor_copy(act_hi[:, i, h], act32[:, i, h]).then_inc(act_hi_done, 1)

            def unscale(src, dst, bias, done):
                dve.scalar_tensor_tensor(out=dst, in0=src[:].rearrange("p (t d) -> p t d", d=D), scalar=INV_W,
                                         in1=row_bias[:, bias:bias + 1, :].broadcast_to([P, 2, D]),
                                         op0=ALU.mult, op1=ALU.add).then_inc(done, 1)

            def add_bias(n, i):
                if known_zero(n):
                    dve.wait_ge(rows_loaded, ROWS)
                for b in range(2):
                    dve.wait_ge(kq2_done, 4 * n + 2 * i + b + 1)
                    if not known_zero(n):
                        dve.wait_ge(kq_lo_done, 2 * n)
                    unscale(side_ps[(2, 0)[i] + b], kqx[:, i, 2 * b:2 * b + 2], 1 + i, kq_biased)

            def gate_bias(n, b):
                dve.wait_ge(gproj_done, 2 * n + b + 1)
                if not known_zero(n):
                    dve.wait_ge(og_done, TT * n)
                unscale(side_ps[b], gate[:, 2 * b:2 * b + 2], 0, gate_biased)

            def finish_kq(n, i):
                dve.wait_ge(softplus_done, 2 * n + i + 1)
                v = flat(kqx[:, i])
                dve.scalar_tensor_tensor(out=v, in0=v, scalar=0.0, in1=soft[:, i], op0=ALU.max,
                                         op1=ALU.add).then_inc(kq_summed, 1)

            def kv_sum(n):
                dve.wait_ge(kv_done, n + 1)
                dve.tensor_tensor(kv[:], side_ps[0][:, 0:D].rearrange("p (h m) -> p h m", h=2),
                                  blockmask[:].unsqueeze(1).broadcast_to([P, 2, P]), ALU.mult).then_inc(kv_masked, 1)

            def kv_norm(n):
                def link(k, ins):
                    ins.then_inc(mix_step, 1)
                    dve.wait_ge(mix_step, MIX_STEPS * n + k)
                dve.wait_ge(z_done, n + 1)
                dve.tensor_scalar(flat(zden[:]), side_ps[1][:, 0:D], ATT_SCALE, float(D), ALU.mult, ALU.add).then_inc(mix_step, 1)
                link(2, dve.scalar_tensor_tensor(out=kvi[:], in0=kv[:], scalar=ATT_SCALE,
                                                 in1=ident[:].unsqueeze(1).broadcast_to([P, 2, P]), op0=ALU.mult, op1=ALU.add))
                link(3, dve.reciprocal(zrec[:], zden[:]))

            def mix_in(n):
                def link(k, ins):
                    ins.then_inc(mix_step, 1)
                    dve.wait_ge(mix_step, MIX_STEPS * n + k)
                link(4, dve.tensor_tensor(mix[:], kvi[:], zrec[:], ALU.mult))
                link(5, dve.tensor_copy(mix_hi[:], mix[:]))
                link(6, dve.tensor_tensor(mix_lo[:], mix[:], mix_hi[:], ALU.subtract))

            def gate_out(n):
                dve.wait_ge(gate_ready, 2 * n + 2)
                for t in range(TT):
                    dve.wait_ge(apply_done, 2 * n + t // 2 + 1)
                    dve.tensor_tensor(og[:, :, :, t, :].rearrange("p a h n -> p h a n"),
                                      down_view(side_ps[2 + t // 2], t), down_view(gate[:, t, :], None),
                                      ALU.mult).then_inc(og_done, 1)

            def down_view(ap, t):
                if t is not None:
                    ap = ap[:, (t % 2) * D:(t % 2 + 1) * D]
                return ap.rearrange("p (h a n) -> p h a n", h=2, n=HD)

            def split_out(n, b):
                dve.wait_ge(ot_hi_done, 2 * n + b + 1)
                for (src, hi), (_, lo) in zip(quarters(b, ot_hi), quarters(b, ot_lo)):
                    ins = dve.tensor_tensor(lo, src, hi, ALU.subtract)
                ins.then_inc(ot_lo_done, 1)

            def residual(n):
                dve.wait_ge(x1b_done, n + 1)
                for h in range(2):
                    dve.wait_ge(project_done, 2 * n + h + 1)
                    dve.scalar_tensor_tensor(out=flat(x2[:, 2 * h:2 * h + 2]), in0=side_ps[2 + h][:], scalar=INV_W,
                                             in1=flat(x1b[:, 2 * h:2 * h + 2]), op0=ALU.mult, op1=ALU.add).then_inc(x2_done, 1)

            pipeline(dve.Fori, dict(small_weights=small_weights, weights=weights, stats=stats, norm=norm, turn_lo=turn_lo, route_scores=route_scores,
                                    route_groups=route_groups,
                                    route_experts=route_experts, route_weights=route_weights, ffn=ffn, finish=finish,
                                    split=split, add_bias=add_bias, gate_bias=gate_bias, finish_kq=finish_kq,
                                    kv_sum=kv_sum, kv_norm=kv_norm, mix=mix_in, gate_out=gate_out, split_out=split_out,
                                    residual=residual))


_INS = ["attn_x", "attn_q_w1", "attn_q_b1", "attn_q_w2", "attn_q_b2", "attn_k_w1", "attn_k_b1", "attn_k_w2",
        "attn_k_b2", "attn_v_w", "attn_v_b", "attn_g_w", "attn_g_b", "attn_p_w", "attn_p_b", "ffn_router_weight",
        "ffn_e_bias", "ffn_gate_w", "ffn_up_w", "ffn_down_w", "ffn_sh_gate_w", "ffn_sh_up_w", "ffn_sh_down_w"]


def kernel(**inputs):
    import numpy as _np
    import concourse.bacc as _bacc
    from concourse import mybir as _mybir
    from concourse.bass_utils import run_bass_kernel_spmd as _run

    nc = _bacc.Bacc("TRN2", target_bir_lowering=False, num_devices=1)
    arrays, args = {}, []
    for name in _INS:
        a = _np.ascontiguousarray(inputs["L0_" + name])
        arrays[f"in_{name}_dram"] = a
        args.append(nc.dram_tensor(f"in_{name}_dram", a.shape, _mybir.dt.from_np(a.dtype), kind="ExternalInput").ap())
    args.append(nc.dram_tensor("out_dram", (SEQS, TOK, D), F32, kind="ExternalOutput").ap())
    macaron(nc, *args)
    ran = _run(nc, [arrays], core_ids=[0])
    return ran.results[0]["out_dram"]
```
